# Optimizing a Trainium2 kernel written in Bass

```python
import numpy as np
import jax
import jax.numpy as jnp

def _softmax(x, axis=-1):
    return jax.nn.softmax(x, axis=axis)

def _gelu(x):
    return jax.nn.gelu(x, approximate=True)

def _silu(x):
    return jax.nn.silu(x)

def _sigmoid(x):
    return jax.nn.sigmoid(x)

def _layernorm(x, axis=-1, eps=1e-05):
    m = jnp.mean(x, axis=axis, keepdims=True)
    v = jnp.var(x, axis=axis, keepdims=True)
    return (x - m) / jnp.sqrt(v + eps)

def _scatter_add(tgt, idx, src, axis=0):
    return tgt.at[idx].add(src)

def _segment_sum(src, seg, n):
    return jax.ops.segment_sum(src, seg, n)
kernel_name = 'mk_decoder_preln_d1_seqx_r4_7b2e3e'

def setup_inputs(seed: int=0):
    np.random.seed(seed)
    _w = jnp.asarray

    def _rec_inputs():
        import jax
        import jax.numpy as jnp
        _rk = jax.random.key(seed)
        x = 7.22e-05 + 1 * jax.random.normal(jax.random.fold_in(_rk, 1), (4, 512, 512), jnp.float32)
        _lenS = 512 - jax.random.randint(jax.random.fold_in(_rk, 7), (4,), 0, max(1, 512 // 4) + 1, jnp.int32)
        _lenS2 = 1601 - jax.random.randint(jax.random.fold_in(_rk, 8), (4,), 0, max(1, 1601 // 4) + 1, jnp.int32)
        _ctx_512P = jax.random.normal(jax.random.fold_in(_rk, 11), (4, 16, 128), jnp.float32)
        _ctx_512c = jax.random.dirichlet(jax.random.fold_in(_rk, 511), 0.3 * jnp.ones((16,), jnp.float32), (4, 1601))
        _ctx_512t = jnp.einsum('bsk,bkd->bsd', _ctx_512c, _ctx_512P)
        _ctx_512t = _ctx_512t * jax.lax.rsqrt(jnp.mean(jnp.square(_ctx_512t)) + 1e-12) * 0.953939
        ctx_512 = -0.000514642 + 1.00011 * (_ctx_512t + 0.3 * jax.random.normal(jax.random.fold_in(_rk, 611), (4, 1601, 128), jnp.float32))
        return (x, ctx_512)
    x, ctx_512 = _rec_inputs()

    def _L0_attn_setup():
        import jax, jax.numpy as jnp
        import numpy as np
        HIDDEN = 512
        NUM_HEADS = 16
        HEAD_DIM = HIDDEN // NUM_HEADS
        WORLD_SIZE = 4
        BATCH = 1
        SEQ_SHARD = 512

        def _ring_attention(q, k, v):
            B, H, S, D = q.shape
            scale = 1.0 / np.sqrt(D)
            output_acc = jnp.zeros_like(q)
            max_score = jnp.full((B, H, S, 1), -jnp.inf, dtype=q.dtype)
            sum_exp = jnp.zeros((B, H, S, 1), dtype=q.dtype)
            for _ in range(WORLD_SIZE):
                scores = jnp.einsum('bhsd,bhtd->bhst', q, k) * scale
                new_max = jnp.max(scores, axis=-1, keepdims=True)
                combined_max = jnp.maximum(max_score, new_max)
                old_scale = jnp.exp(max_score - combined_max)
                new_scale = jnp.exp(new_max - combined_max)
                new_exp = jnp.exp(scores - new_max)
                sum_exp = sum_exp * old_scale + jnp.sum(new_exp, axis=-1, keepdims=True) * new_scale
                output_acc = output_acc * old_scale + jnp.einsum('bhst,bhtd->bhsd', new_exp, v) * new_scale
                max_score = combined_max
            return output_acc / sum_exp
        key = jax.random.key(seed)
        ks = jax.random.split(key, 9)
        s = 1.0 / np.sqrt(HIDDEN)
        return {'hidden_states': jax.random.normal(ks[0], (BATCH, SEQ_SHARD, HIDDEN), jnp.float32), 'wq': jax.random.normal(ks[1], (HIDDEN, HIDDEN), jnp.float32) * s, 'bq': jax.random.normal(ks[2], (HIDDEN,), jnp.float32) * s, 'wk': jax.random.normal(ks[3], (HIDDEN, HIDDEN), jnp.float32) * s, 'bk': jax.random.normal(ks[4], (HIDDEN,), jnp.float32) * s, 'wv': jax.random.normal(ks[5], (HIDDEN, HIDDEN), jnp.float32) * s, 'bv': jax.random.normal(ks[6], (HIDDEN,), jnp.float32) * s, 'wo': jax.random.normal(ks[7], (HIDDEN, HIDDEN), jnp.float32) * s, 'bo': jax.random.normal(ks[8], (HIDDEN,), jnp.float32) * s}
    _L0_attn_all = _L0_attn_setup()
    _L0_attn_in = {k: v for k, v in _L0_attn_all.items() if k in ('wq', 'bq', 'wk', 'bk', 'wv', 'bv', 'wo', 'bo')}
    del _L0_attn_all

    def _L0_xattn_setup():
        import jax, jax.numpy as jnp
        import numpy as np
        B, S, H, NH, L = (2, 512, 512, 16, 128)
        HD = H // NH
        key = jax.random.key(seed)
        k1, k2, k3, k4, k5 = jax.random.split(key, 5)
        scale = 0.02
        return {'q': jax.random.normal(k1, (B, S, H), dtype=jnp.float32), 'latent_kv': jax.random.normal(k2, (B, S, L), dtype=jnp.float32), 'Wq': jax.random.normal(k3, (H, H), dtype=jnp.float32) * scale, 'Wkv_expand': jax.random.normal(k4, (2 * H, L), dtype=jnp.float32) * scale, 'Wout': jax.random.normal(k5, (H, H), dtype=jnp.float32) * scale}
    _L0_xattn_all = _L0_xattn_setup()
    _L0_xattn_in = {k: v for k, v in _L0_xattn_all.items() if k in ('Wq', 'Wkv_expand', 'Wout')}
    del _L0_xattn_all

    def _L0_ffn_setup():
        import jax, jax.numpy as jnp
        import numpy as np
        L, N, E, H, K = (512, 8, 512, 2048, 8)
        key = jax.random.key(seed)
        ks = jax.random.split(key, 6)
        return {'x': jax.random.normal(ks[0], (L, N, E), dtype=jnp.float32), 'proj1': jax.random.normal(ks[1], (H, E), dtype=jnp.float32) * 0.02, 'proj1_bias': jax.random.normal(ks[2], (H,), dtype=jnp.float32) * 0.02, 'proj2': jax.random.normal(ks[3], (E, H), dtype=jnp.float32) * 0.02, 'proj2_bias': jax.random.normal(ks[4], (E,), dtype=jnp.float32) * 0.02, 'gate_w': jax.random.normal(ks[5], (E, K), dtype=jnp.float32)}
    _L0_ffn_all = _L0_ffn_setup()
    _L0_ffn_in = {k: v for k, v in _L0_ffn_all.items() if k in ('proj1', 'proj1_bias', 'proj2', 'proj2_bias', 'gate_w')}
    del _L0_ffn_all
    return {'x': x, 'ctx_512': ctx_512, 'L0_attn_wq': _L0_attn_in['wq'], 'L0_attn_bq': _L0_attn_in['bq'], 'L0_attn_wk': _L0_attn_in['wk'], 'L0_attn_bk': _L0_attn_in['bk'], 'L0_attn_wv': _L0_attn_in['wv'], 'L0_attn_bv': _L0_attn_in['bv'], 'L0_attn_wo': _L0_attn_in['wo'], 'L0_attn_bo': _L0_attn_in['bo'], 'L0_xattn_Wq': _L0_xattn_in['Wq'], 'L0_xattn_Wkv_expand': _L0_xattn_in['Wkv_expand'], 'L0_xattn_Wout': _L0_xattn_in['Wout'], 'L0_ffn_proj1': _L0_ffn_in['proj1'], 'L0_ffn_proj1_bias': _L0_ffn_in['proj1_bias'], 'L0_ffn_proj2': _L0_ffn_in['proj2'], 'L0_ffn_proj2_bias': _L0_ffn_in['proj2_bias'], 'L0_ffn_gate_w': _L0_ffn_in['gate_w']}

def reference(x, ctx_512, L0_attn_wq, L0_attn_bq, L0_attn_wk, L0_attn_bk, L0_attn_wv, L0_attn_bv, L0_attn_wo, L0_attn_bo, L0_xattn_Wq, L0_xattn_Wkv_expand, L0_xattn_Wout, L0_ffn_proj1, L0_ffn_proj1_bias, L0_ffn_proj2, L0_ffn_proj2_bias, L0_ffn_gate_w):
    import jax
    import jax.numpy as jnp

    def _L0_attn_ref(hidden_states, wq, bq, wk, bk, wv, bv, wo, bo):
        import jax, jax.numpy as jnp
        import numpy as np
        HIDDEN = 512
        NUM_HEADS = 16
        HEAD_DIM = HIDDEN // NUM_HEADS
        WORLD_SIZE = 4
        BATCH = 1
        SEQ_SHARD = 512

        def _ring_attention(q, k, v):
            B, H, S, D = q.shape
            scale = 1.0 / np.sqrt(D)
            output_acc = jnp.zeros_like(q)
            max_score = jnp.full((B, H, S, 1), -jnp.inf, dtype=q.dtype)
            sum_exp = jnp.zeros((B, H, S, 1), dtype=q.dtype)
            for _ in range(WORLD_SIZE):
                scores = jnp.einsum('bhsd,bhtd->bhst', q, k) * scale
                new_max = jnp.max(scores, axis=-1, keepdims=True)
                combined_max = jnp.maximum(max_score, new_max)
                old_scale = jnp.exp(max_score - combined_max)
                new_scale = jnp.exp(new_max - combined_max)
                new_exp = jnp.exp(scores - new_max)
                sum_exp = sum_exp * old_scale + jnp.sum(new_exp, axis=-1, keepdims=True) * new_scale
                output_acc = output_acc * old_scale + jnp.einsum('bhst,bhtd->bhsd', new_exp, v) * new_scale
                max_score = combined_max
            return output_acc / sum_exp
        B, S, _ = hidden_states.shape
        q = hidden_states @ wq.T + bq
        k = hidden_states @ wk.T + bk
        v = hidden_states @ wv.T + bv
        split = lambda t: t.reshape(B, S, NUM_HEADS, HEAD_DIM).transpose(0, 2, 1, 3)
        attn = _ring_attention(split(q), split(k), split(v))
        attn = attn.transpose(0, 2, 1, 3).reshape(B, S, HIDDEN)
        return attn @ wo.T + bo

    def _L0_xattn_ref(q, latent_kv, Wq, Wkv_expand, Wout):
        import jax, jax.numpy as jnp
        import numpy as np
        B, S, H, NH, L = (2, 512, 512, 16, 128)
        HD = H // NH
        b, sq, _ = q.shape
        sk = latent_kv.shape[1]
        qp = q @ Wq.T
        kv = latent_kv @ Wkv_expand.T
        k, v = jnp.split(kv, 2, axis=-1)
        qh = qp.reshape(b, sq, NH, HD).transpose(0, 2, 1, 3)
        kh = k.reshape(b, sk, NH, HD).transpose(0, 2, 1, 3)
        vh = v.reshape(b, sk, NH, HD).transpose(0, 2, 1, 3)
        inv_sqrt_d = 1.0 / jnp.sqrt(jnp.float32(HD))
        scores = jnp.einsum('bhqd,bhkd->bhqk', qh, kh) * inv_sqrt_d
        causal = jnp.tril(jnp.ones((sq, sk), dtype=bool))
        scores = jnp.where(causal, scores, jnp.finfo(scores.dtype).min)
        attn = jax.nn.softmax(scores, axis=-1)
        out = jnp.einsum('bhqk,bhkd->bhqd', attn, vh)
        out = out.transpose(0, 2, 1, 3).reshape(b, sq, H)
        return out @ Wout.T

    def _L0_ffn_ref(x, proj1, proj1_bias, proj2, proj2_bias, gate_w):
        import jax, jax.numpy as jnp
        import numpy as np
        L, N, E, H, K = (512, 8, 512, 2048, 8)
        dst = jnp.argmax(jnp.einsum('lne,ek->lnk', x, gate_w), axis=-1)
        h = jax.nn.gelu(jnp.einsum('lne,he->lnh', x, proj1) + proj1_bias, approximate=False)
        out = jnp.einsum('lnh,eh->lne', h, proj2) + proj2_bias
        del dst
        return out
    x = x + _L0_attn_ref(_layernorm(x, axis=-1), L0_attn_wq, L0_attn_bq, L0_attn_wk, L0_attn_bk, L0_attn_wv, L0_attn_bv, L0_attn_wo, L0_attn_bo)
    x = x + _L0_xattn_ref(_layernorm(x, axis=-1), ctx_512, L0_xattn_Wq, L0_xattn_Wkv_expand, L0_xattn_Wout)
    x = x + _L0_ffn_ref(_layernorm(x, axis=-1), L0_ffn_proj1, L0_ffn_proj1_bias, L0_ffn_proj2, L0_ffn_proj2_bias, L0_ffn_gate_w)
    return x

_drawn_inputs = setup_inputs


def setup_inputs(seed=0):
    import zlib

    import numpy as np

    out = dict(_drawn_inputs(seed))
    spreads = {}
    factors = {'L0_attn_bq': 8.0,
     'L0_attn_bk': 64.0,
     'L0_xattn_Wq': 25.251,
     'L0_ffn_proj1_bias': 5.396,
     'L0_ffn_proj2_bias': 3.045}
    for name, (base, spread) in spreads.items():
        noise = np.random.default_rng([zlib.crc32(name.encode()), seed]).standard_normal(out[name].shape)
        drawn = base * np.exp(spread * noise) if base else spread * noise
        out[name] = jnp.asarray(drawn.astype(out[name].dtype))
    for name, factor in factors.items():
        out[name] = (out[name] * factor).astype(out[name].dtype)
    return out
```

```python
from contextlib import ExitStack

import concourse.bass as bass
from concourse import mybir

F32 = mybir.dt.float32
F32R = mybir.dt.float32r
BF16 = mybir.dt.bfloat16
ALU = mybir.AluOpType
ACT = mybir.ActivationFunctionType
AX = mybir.AxisListType

P = 128
BATCH = 4
SEQ = 512
DIM = 512
HEAD = 32
LATENT = 128
HIDDEN = 2048
KT = DIM // P
GROUPS = 4
HPG = 4
SELF, CROSS = 0, 1
WQ, WK, WV, WO = range(4)
WKV2, WO2, WQ2 = 0, 1, 2
CTX_SLICE = 2
CHUNKS = HIDDEN // P
CHUNK = 2 * DIM
CHUNK_ORDER = [6, 7, 4, 5, 0, 1, 2, 3] + list(range(8, CHUNKS))
STACK = 3 * HEAD
SCALE = float(HEAD) ** -0.5
EPS = 1e-5
MASKED = -1e30
EARLY = 3
SMALL = 5
DMA = 16
LAST = 2 * BATCH - 1
STACKED = 24 * DMA
MAXED = 2 * DMA


def decoder_layer(nc, x, ctxT, wT, bq, bk, bv, bo, wq2T, wkv2T, wo2T, p1T, b1, p2T, b2, out):
    x_t = x.rearrange("b (t p) n -> b p t n", p=P)
    out_t = out.rearrange("b (t p) n -> b p t n", p=P)

    ctx = ExitStack()
    with ctx:
        def sem(name):
            return ctx.enter_context(nc.semaphore(name))

        def sb(name, shape, dt, scope=ctx):
            return scope.enter_context(nc.sbuf_tensor(name, shape, dt))

        x_res = sb("x_res", [P, BATCH * KT, DIM], F32)
        xn = sb("xn", [P, 2, DIM], F32)
        raw = sb("raw", [P, CHUNK], F32)
        ident = sb("ident", [P, P], F32)
        ones = sb("ones", [P, HEAD], F32)
        identb = sb("identb", [P, P], BF16)
        mask_qk = sb("mask_qk", [P, P], BF16)
        mask_kq = sb("mask_kq", [P, P], BF16)
        stats = sb("stats", [P, KT, 6], F32)
        mv = sb("mv", [P, KT, 2], F32)
        veps = sb("veps", [P, KT], F32)
        rstd = sb("rstd", [P, KT], F32)
        mhalf = sb("mhalf", [P, KT], F32)
        spare = sb("spare", [P, 1], F32)
        epsc = sb("epsc", [P, KT], F32)
        b1c = sb("b1c", [P, CHUNKS], F32)
        bqc = sb("bqc", [P, GROUPS], F32)
        bkc = sb("bkc", [P, GROUPS], F32)
        m_cols = sb("m_cols", [P, HPG * KT], F32)

        attn = ExitStack()
        WH = sb("WH", [P, 4, KT, DIM], F32R, attn)
        stackQ = sb("stackQ", [P, 2, HPG, SEQ], F32R, attn)
        stackK = sb("stackK", [P, 2, HPG, SEQ], F32R, attn)
        WL = sb("WL", [P, 4, KT, DIM], F32R, attn)
        xTH = sb("xTH", [P, KT, SEQ], F32R, attn)
        xTL = sb("xTL", [P, KT, SEQ], F32R, attn)
        oTH = sb("oTH", [P, GROUPS, SEQ], F32R, attn)
        oTL = sb("oTL", [P, GROUPS, SEQ], F32R, attn)
        stH = sb("stH", [P, SEQ], F32R, attn)
        stL = sb("stL", [P, SEQ], F32R, attn)
        m_row = sb("m_row", [HPG * KT, 2, P], F32R, attn)
        V = sb("V", [P, KT, DIM], F32, attn)
        PT = sb("PT", [P, 8, SEQ], F32, attn)
        oT = sb("oT", [P, SEQ], F32, attn)
        bv_b = sb("bv_b", [P, DIM], F32, attn)
        bo_b = sb("bo_b", [P, DIM], F32, attn)
        attn.close()
        ffn = ExitStack()
        FH = sb("FH", [P, CHUNKS, CHUNK], F32R, ffn)
        FL = sb("FL", [P, CHUNKS, CHUNK], F32R, ffn)
        fTH = sb("fTH", [P, KT, SEQ], F32R, ffn)
        fTL = sb("fTL", [P, KT, SEQ], F32R, ffn)
        hid = sb("hid", [P, 2, SEQ], F32, ffn)
        hidH = sb("hidH", [P, 2, SEQ], F32R, ffn)
        hidL = sb("hidL", [P, 2, SEQ], F32R, ffn)
        b2_b = sb("b2_b", [P, DIM], F32, ffn)
        raw2 = sb("raw2", [P, CHUNK], F32, ffn)
        ffn.close()

        PS = ctx.enter_context(nc.psum_tensor("PS", [P, 8, 512], F32))
        S_BANK, T_BANK, O_BANK, R_BANK, G_BANK = 0, 2, 4, 5, 6
        ACC_BANK, H_BANK = 0, 4

        x_loaded = sem("x_loaded")
        small_loaded = sem("small_loaded")
        w_loaded = [sem(f"w_loaded{m}") for m in range(4)]
        consts = sem("consts")
        wH_ready = sem("wH_ready")
        w_ready = sem("w_ready")
        raw_loaded = sem("raw_loaded")
        raw_high = sem("raw_high")
        raw_split = sem("raw_split")
        spare_done = sem("spare_done")
        stats_done = sem("stats_done")
        mv_done = sem("mv_done")
        veps_done = sem("veps_done")
        rstd_done = sem("rstd_done")
        xn_done = sem("xn_done")
        bo_added = sem("bo_added")
        g_full = sem("g_full")
        g_high = sem("g_high")
        g_done = sem("g_done")
        stack_in = [sem("stack_in0"), sem("stack_in1")]
        m_high = sem("m_high")
        m_in = [sem("m_in0"), sem("m_in1")]
        s_full = sem("s_full")
        s_done = sem("s_done")
        t_full = sem("t_full")
        p_ready = sem("p_ready")
        p_used = sem("p_used")
        r_done = sem("r_done")
        o_done = sem("o_done")
        oH_done = sem("oH_done")
        oL_done = sem("oL_done")
        fw_loaded = [sem("fw_loaded0"), sem("fw_loaded1")]
        fwH_ready = sem("fwH_ready")
        fw_ready = sem("fw_ready")
        f_full = sem("f_full")
        f_high = sem("f_high")
        f_done = sem("f_done")
        h_full = sem("h_full")
        h_gelu = sem("h_gelu")
        h_high = sem("h_high")
        h_ready = sem("h_ready")
        h_used = sem("h_used")
        y_done = sem("y_done")
        b2_loaded = sem("b2_loaded")
        b2_added = sem("b2_added")
        out_stored = sem("out_stored")

        def use(b, k):
            if isinstance(b, int) and b == 0 and k < 2:
                return 11 + k
            if isinstance(b, int) and b < 0:
                return {12: 0, 13: 1, 14: 2, 15: 3, 16: 4, 18: 5, 19: 6, 20: 7, 21: 8, 22: 9, 23: 10}[k]
            if isinstance(b, int) and b == LAST and k > 11:
                return b * 24 + (7 + 12)
            if isinstance(b, int) and b > LAST:
                return LAST * 24 + (7 + 13) + (k - 2)
            return b * 24 + (7 + k)

        def bank(k, b=1):
            if isinstance(b, int):
                return G_BANK + use(b, k) % 2
            return G_BANK + (7 + k) % 2

        def use_xT(b, t):
            return b - 1, 12 + t

        def use_Q(b, g):
            return [(b - 1, 16), (b - 1, 19), (b, 6), (b, 9)][g]

        def use_K(b, g):
            return [(b - 1, 18), (b - 1, 21), (b, 8), (b, 11)][g]

        def use_m(b, g):
            return [(b - 1, 20), (b, 7), (b, 10), (b, 17)][g]

        def use_V(b, t):
            return [(b - 1, 22), (b - 1, 23), (b, 0), (b, 1)][t]

        def use_Wo(b, t):
            return b + 1, 2 + t

        def units(b, g):
            return b * GROUPS + g

        def high_count(b, k):
            return b * 12 + (8 + {6: 1, 8: 2, 9: 3, 11: 4, 12: 5, 13: 6, 14: 7, 15: 8, 16: 9, 18: 10, 19: 11, 21: 12}[k])

        def G(n):
            return PS[:, bank(n[1], n[0]), :]

        def F(t):
            return PS[:, G_BANK + t % 2, :]

        def residual(row):
            return x_res[:, bass.ds(row, 1), :].rearrange("p o n -> p (o n)")

        def fraw(i):
            return (raw, raw2)[i % 2][:, :]

        def preceding(b, g):
            return (b, g - 1) if g else (b - 1, GROUPS - 1)

        def following(b, g, d):
            return (b, g + d) if g + d < GROUPS else (b + 1, g + d - GROUPS)

        def batches(eng, slot):
            slot(0, 0, SELF, SELF)
            with eng.Fori(0, BATCH - 1) as b:
                for g in range(1, GROUPS):
                    slot(b, g, SELF, SELF)
                slot(b + 1, 0, SELF, SELF)
            for g in range(1, GROUPS):
                slot(BATCH - 1, g, SELF, CROSS)
            slot(BATCH, 0, CROSS, CROSS)
            with eng.Fori(BATCH, 2 * BATCH - 1) as b:
                for g in range(1, GROUPS):
                    slot(b, g, CROSS, CROSS)
                slot(b + 1, 0, CROSS, CROSS)
            for g in range(1, GROUPS):
                slot(2 * BATCH - 1, g, CROSS, None)

        def queries(layer, k):
            return k * P if layer == CROSS else 0

        def keys(layer, q):
            return (q + 1) * P if layer == CROSS else SEQ

        RAW = []
        for k in range(KT):
            RAW.append(((BATCH - 1, 1), [(raw[:, 0:DIM], wq2T[k * P:(k + 1) * P, :])],
                        WH[:, WQ2, k, :], WL[:, WQ2, k, :], use(*use_V(BATCH - 1, 3)) + 1))
        for k in range(2):
            RAW.append(((BATCH - 1, 2), [(raw[:, 0:DIM], wkv2T[:, k * DIM:(k + 1) * DIM])],
                        WH[:, WKV2, k, :], WL[:, WKV2, k, :], use(*use_K(BATCH - 1, 3)) + 1))
        RAW.append(((BATCH - 1, 2), [(raw[:, 0:SEQ], ctxT[0, :, 0:SEQ])],
                    WH[:, 0, CTX_SLICE, :], WL[:, 0, CTX_SLICE, :], use(*use_K(BATCH - 1, 3)) + 1))
        FIRST_CTX = len(RAW)
        for k in range(KT):
            RAW.append(((BATCH - 1, 3), [(raw[:, 0:DIM], wo2T[k * P:(k + 1) * P, :])],
                        WH[:, WO2, k, :], WL[:, WO2, k, :], use(*use_K(BATCH - 1, 3)) + 1))
        CTX_FROM = len(RAW)
        CTX_OFFSET = CTX_FROM - BATCH

        def chunk_loads(i, buf):
            j = CHUNK_ORDER[i]
            return [(buf[:, 0:DIM].rearrange("p (k n) -> p k n", k=KT),
                     p1T.rearrange("(k p) n -> p k n", p=P)[:, :, j * P:(j + 1) * P]),
                    (buf[:, DIM:CHUNK], p2T[j * P:(j + 1) * P, :])]

        for i in range(EARLY):
            free = use(BATCH, 5) if i < 2 else use(2 * BATCH - 1, 9)
            RAW.append(((2 * BATCH - 1, 1 + i), chunk_loads(i, raw),
                        FH[:, CHUNK_ORDER[i], :], FL[:, CHUNK_ORDER[i], :], free + 1))
        RAW_TOTAL = len(RAW) + BATCH - 1

        def raw_count(n):
            chunks = n - (RAW_TOTAL - EARLY) + 1 if isinstance(n, int) else 0
            return (n + 1 + max(0, chunks)) * DMA if isinstance(n, int) else n * DMA + DMA

        block = ctx.enter_context(nc.Block())

        @block.sync
        def _(sp):
            sp.dma_start(x_res[:, 0:KT, :], x_t[0]).then_inc(x_loaded, DMA)
            for m, buf in ((WQ, PT[:, 0:4, :]), (WK, PT[:, 4:8, :]), (WV, V[:, :, :])):
                sp.dma_start(buf, wT[m].rearrange("(k p) n -> p k n", p=P)).then_inc(w_loaded[m], DMA)
            sp.wait_ge(w_ready, KT)
            sp.dma_start(PT[:, 0:4, :], wT[WO].rearrange("(k p) n -> p k n", p=P)).then_inc(w_loaded[WO], DMA)

            def store_stack(b, g, is_k):
                par = g % 2
                dst = stackK if is_k else stackQ
                sp.wait_ge(g_done, use(*(use_K if is_k else use_Q)(b, g)) + 1)
                for h in range(HPG):
                    rows = slice(HEAD * h, HEAD * h + HEAD)
                    parts = (stH, stH, stL) if is_k else (stH, stL, stH)
                    for j, part in enumerate(parts):
                        sp.dma_start(dst[HEAD * j:HEAD * j + HEAD, par, h, :].bitcast(F32),
                                     part[rows, :].bitcast(F32)).then_inc(stack_in[par], DMA)

            def store_max(b, g):
                par = g % 2
                sp.wait_ge(g_done, use(*use_m(b, g)) + 1)
                for j in range(2):
                    sp.dma_start(stackQ[STACK + j:STACK + j + 1, par, :, :].bitcast(F32).rearrange("o h n -> o (h n)"),
                                 m_row[:, j, :].bitcast(F32)).then_inc(m_in[par], DMA)

            store_stack(0, 0, False)
            store_stack(0, 0, True)
            store_stack(0, 1, False)
            store_max(0, 0)
            store_stack(0, 1, True)

            def slot(b, g, layer, after):
                last_batch = after is None
                if g == 1 and layer == SELF and after == SELF:
                    sp.dma_start(x_res[:, bass.ds(b * KT + KT, KT), :],
                                 x_t[bass.ds(b + 1, 1)].rearrange("o p t n -> (o p) t n")).then_inc(x_loaded, DMA)
                if not (last_batch and g >= 2):
                    store_stack(*following(b, g, 2), False)
                if not (last_batch and g == 3):
                    store_max(*following(b, g, 1))
                if not (last_batch and g >= 2):
                    store_stack(*following(b, g, 2), True)

            batches(sp, slot)

            sp.wait_ge(f_full, 1)
            sp.dma_start(b2_b[:, :], b2).then_inc(b2_loaded, DMA)
            for i in range(EARLY, CHUNKS):
                if i == EARLY + 1:
                    sp.wait_ge(raw_split, RAW_TOTAL)
                elif i > EARLY + 1:
                    sp.wait_ge(fw_ready, i - 1 - EARLY)
                for dst, src in chunk_loads(i, fraw(i)):
                    sp.dma_start(dst, src).then_inc(fw_loaded[i % 2], DMA)

            with sp.Fori(0, BATCH) as b:
                sp.wait_ge(y_done, b * KT + KT)
                sp.dma_start(out_t[bass.ds(b, 1)].rearrange("o p t n -> (o p) t n"),
                             x_res[:, bass.ds(b * KT, KT), :]).then_inc(out_stored, DMA)
            sp.wait_ge(out_stored, DMA * BATCH)

        @block.gpsimd
        def _(pool):
            pool.memset(ident[:, :], 0.0).then_inc(consts, 1)
            pool.memset(identb[:, :], 0.0).then_inc(consts, 1)
            pool.memset(mask_qk[:, :], 0.0).then_inc(consts, 1)
            pool.memset(mask_kq[:, :], 0.0).then_inc(consts, 1)
            pool.memset(mhalf[:, :], -0.5).then_inc(consts, 1)
            pool.memset(epsc[:, :], EPS).then_inc(consts, 1)
            pool.memset(ones[:, :], 1.0).then_inc(consts, 1)
            pool.wait_ge(consts, 7)
            pool.memset(stackK[STACK:STACK + 2, :, :, :].bitcast(F32), 1.0).then_inc(consts, 1)
            pool.wait_ge(consts, 8)
            for t in (ident, identb):
                pool.affine_select(out=t[:, :], in_=t[:, :], compare_op=ALU.not_equal, fill=1.0,
                                   base=0, pattern=[[-1, P]], channel_multiplier=1).then_inc(consts, 1)
            pool.affine_select(out=mask_qk[:, :], in_=mask_qk[:, :], compare_op=ALU.is_ge, fill=MASKED,
                               base=0, pattern=[[-1, P]], channel_multiplier=1).then_inc(consts, 1)
            pool.affine_select(out=mask_kq[:, :], in_=mask_kq[:, :], compare_op=ALU.is_ge, fill=MASKED,
                               base=0, pattern=[[1, P]], channel_multiplier=-1).then_inc(consts, 1)

            def root(b):
                pool.wait_ge(mv_done, b * KT + KT)
                pool.tensor_tensor(veps[:, :], mv[:, :, 1], epsc[:, :], ALU.add).then_inc(veps_done, 1)
                pool.wait_ge(veps_done, b + 1)
                pool.tensor_tensor(rstd[:, :], veps[:, :], mhalf[:, :], ALU.pow).then_inc(rstd_done, 1)

            def add_bo(b):
                for t in range(KT):
                    pool.wait_ge(xn_done, b * KT + (t + 1))
                    tile = residual(b * KT + t)
                    pool.tensor_tensor(tile, tile, bo_b[:, :], ALU.add).then_inc(bo_added, 1)

            def load_raw(n, src, low, high):
                if not (isinstance(n, int) and n == 0):
                    pool.wait_ge(raw_split, n)
                width = 1
                for d in low.shape[1:]:
                    width *= d
                for dst, part in src:
                    pool.dma_start(dst, part).then_inc(raw_loaded, DMA)
                pool.wait_ge(raw_high, n + 1)
                pool.tensor_tensor(low, raw[:, 0:width], high.bitcast(F32), ALU.subtract).then_inc(raw_split, 1)

            def low_output(b, g):
                pool.wait_ge(oH_done, units(b, g) + 1)
                pool.tensor_tensor(oTL[:, g, :], oT[:, :], oTH[:, g, :].bitcast(F32),
                                   ALU.subtract).then_inc(oL_done, 1)

            root(0)
            pool.wait_ge(small_loaded, DMA * SMALL)
            add_bo(0)

            def slot(b, g, layer, after):
                if g == 2 and after is not None:
                    root(b + 1)
                if not (isinstance(b, int) and b == 0 and g == 0):
                    low_output(*preceding(b, g))
                if g == 3 and after == SELF:
                    add_bo(b + 1)
                for n, (at, src, high, low, _) in enumerate(RAW):
                    if at == (b if isinstance(b, int) else -1, g):
                        load_raw(n if n < CTX_FROM else n + BATCH - 1, src, low, high)
                if g == 2 and layer == CROSS and after == CROSS:
                    load_raw(b + CTX_OFFSET,
                             [(raw[:, 0:SEQ], ctxT[bass.ds(b + (1 - BATCH), 1), :, 0:SEQ].rearrange("o p n -> (o p) n"))],
                             WL[:, 0, CTX_SLICE, :], WH[:, 0, CTX_SLICE, :])

            batches(pool, slot)
            low_output(2 * BATCH - 1, GROUPS - 1)

            def ffn_norm(b):
                root(b + 2 * BATCH)
                for t in range(KT):
                    pool.wait_ge(xn_done, b * KT + (2 * BATCH * KT + t + 1))
                    tile = residual(b * KT + t)
                    pool.tensor_tensor(tile, tile, b2_b[:, :], ALU.add).then_inc(b2_added, 1)

            root(2 * BATCH)
            pool.wait_ge(b2_loaded, DMA)
            for t in range(KT):
                pool.wait_ge(xn_done, 2 * BATCH * KT + t + 1)
                pool.tensor_tensor(x_res[:, t, :], x_res[:, t, :], b2_b[:, :], ALU.add).then_inc(b2_added, 1)
            with pool.Fori(1, BATCH) as b:
                ffn_norm(b)

        @block.scalar
        def _(act):
            for dst, src in ((bqc[:, :], bq), (bkc[:, :], bk), (bv_b[:, :], bv), (bo_b[:, :], bo), (b1c[:, :], b1)):
                act.dma_start(dst, src).then_inc(small_loaded, DMA)

            def high_weight(m, buf):
                act.wait_ge(w_loaded[m], DMA)
                for k in range(KT):
                    nc.scalar.activation(WH[:, m, k, :], buf[:, k, :], ACT.Copy).then_inc(wH_ready, 1)

            def high_xT(b, t):
                n = use_xT(b, t)
                act.wait_ge(g_full, use(*n) + 1)
                nc.scalar.activation(xTH[:, :, t * P:(t + 1) * P],
                                     G(n).rearrange("p (k n) -> p k n", k=KT), ACT.Copy).then_inc(g_high, 1)

            def high_QK(b, g, is_k, layer):
                n = (use_K if is_k else use_Q)(b, g)
                act.wait_ge(g_full, use(*n) + 1)
                if is_k:
                    act.wait_ge(stack_in[g % 2], b * (2 * STACKED) + (STACKED * (g // 2) + STACKED // 2))
                elif not (isinstance(b, int) and b == 0 and g == 0):
                    pb, pg = preceding(b, g)
                    act.wait_ge(stack_in[pg % 2], pb * (2 * STACKED) + STACKED * (pg // 2 + 1))
                if layer == SELF:
                    nc.scalar.activation(stH[:, :], G(n), ACT.Identity,
                                         bias=(bkc if is_k else bqc)[:, g:g + 1]).then_inc(g_high, 1)
                else:
                    nc.scalar.activation(stH[:, :], G(n), ACT.Copy).then_inc(g_high, 1)

            def high_output(b, g):
                act.wait_ge(o_done, units(b, g) + 1)
                if g == 0:
                    act.wait_ge(g_full, b * 24 + (7 + 6))
                nc.scalar.activation(oTH[:, g, :], oT[:, :], ACT.Copy).then_inc(oH_done, 1)

            def high_raw(n, high, free):
                act.wait_ge(g_full, free)
                act.wait_ge(raw_loaded, raw_count(n))
                width = 1
                for d in high.shape[1:]:
                    width *= d
                nc.scalar.activation(high, raw[:, 0:width], ACT.Copy).then_inc(raw_high, 1)

            high_weight(WQ, PT[:, 0:4, :])
            for t in range(KT):
                high_xT(0, t)
            high_weight(WK, PT[:, 4:8, :])
            act.wait_ge(small_loaded, DMA * SMALL)
            high_QK(0, 0, False, SELF)
            high_QK(0, 0, True, SELF)
            high_weight(WV, V)
            high_QK(0, 1, False, SELF)
            high_QK(0, 1, True, SELF)
            high_weight(WO, PT[:, 0:4, :])
            act.wait_ge(w_ready, 4 * KT)

            def slot(b, g, layer, after):
                raws = [(n if n < CTX_FROM else n + BATCH - 1, high, free)
                        for n, (at, _, high, _, free) in enumerate(RAW)
                        if at == (b if isinstance(b, int) else -1, g)]
                if g == 2 and layer == CROSS and after == CROSS:
                    raws = [(b + CTX_OFFSET, WH[:, 0, CTX_SLICE, :], use(*use_K(b, GROUPS - 1)) + 1)]
                for k in range(KT):
                    if not (isinstance(b, int) and b == 0 and g == 0 and k < 2):
                        act.wait_ge(p_used, b * 16 + (4 * g + k - 1))
                    for h in range(HPG):
                        act.wait_ge(t_full, b * 64 + (16 * g + 4 * k + h + 1))
                        q0 = queries(layer, k)
                        nc.scalar.activation(PT[:, (4 * k + h) % 8, q0:SEQ], PS[:, T_BANK + h % 2, q0:SEQ],
                                             ACT.Exp, scale=SCALE).then_inc(p_ready, 1)
                    if k == 0 and not (isinstance(b, int) and b == 0 and g == 0):
                        high_output(*preceding(b, g))
                    if g == 2 and after is not None:
                        high_xT(b + 1, k)
                    if k < len(raws):
                        high_raw(*raws[k])
                nb, ng = following(b, g, 2)
                if g < 2 or after is not None:
                    high_QK(nb, ng, False, layer if g < 2 else after)
                    high_QK(nb, ng, True, layer if g < 2 else after)

            batches(act, slot)
            high_output(2 * BATCH - 1, GROUPS - 1)

            def high_fT(b, t):
                act.wait_ge(f_full, b * KT + (t + 1))
                nc.scalar.activation(fTH[:, :, t * P:(t + 1) * P],
                                     F(t).rearrange("p (k n) -> p k n", k=KT), ACT.Copy).then_inc(f_high, 1)

            def gelu(b, i):
                act.wait_ge(h_full, b * CHUNKS + (i + 1))
                if not (isinstance(b, int) and b == 0 and i < 2):
                    act.wait_ge(h_ready, b * CHUNKS + (i - 1))
                j = CHUNK_ORDER[i]
                nc.scalar.activation(hid[:, i % 2, :], PS[:, H_BANK + i % 2, :], ACT.Gelu,
                                     bias=b1c[:, j:j + 1]).then_inc(h_gelu, 1)

            def high_chunk(i):
                act.wait_ge(fw_loaded[i % 2], DMA * 2 * ((i - EARLY) // 2 + 1))
                nc.scalar.activation(FH[:, CHUNK_ORDER[i], :], fraw(i), ACT.Copy).then_inc(fwH_ready, 1)

            for t in range(KT):
                high_fT(0, t)
            for i in range(CHUNKS):
                if i + 3 < CHUNKS:
                    high_chunk(i + 3)
                gelu(0, i)
            for t in range(KT):
                high_fT(1, t)
            with act.Fori(1, BATCH - 1) as b:
                for i in range(CHUNKS):
                    gelu(b, i)
                for t in range(KT):
                    high_fT(b + 1, t)
            for i in range(CHUNKS):
                gelu(BATCH - 1, i)

        @block.tensor
        def _(pe):
            def product(dst, wH, wL, mH, mL, first, last):
                nc.tensor.matmul(dst, wH, mH, start=first, stop=False)
                nc.tensor.matmul(dst, wH, mL, start=False, stop=False)
                return nc.tensor.matmul(dst, wL, mH, start=False, stop=last)

            def take_bank(n):
                if not (isinstance(n[0], int) and use(*n) < 2):
                    pe.wait_ge(g_done, use(*n) - 1)

            def transpose_x(b, t):
                n = use_xT(b, t)
                take_bank(n)
                pe.wait_ge(xn_done, b * KT + (t + 1))
                for k in range(KT):
                    mm = nc.tensor.transpose(G(n)[:, k * P:(k + 1) * P], xn[:, t % 2, k * P:(k + 1) * P], ident[:, :])
                mm.then_inc(g_full, 1)

            def project_QK(b, g, is_k, layer):
                n = (use_K if is_k else use_Q)(b, g)
                take_bank(n)
                if g == 0:
                    pe.wait_ge(g_done, use(*use_xT(b, KT - 1)) + 1)
                cols = slice(g * P, (g + 1) * P)
                if layer == CROSS and is_k:
                    if g == 0:
                        pe.wait_ge(raw_split, FIRST_CTX if isinstance(b, int) and b == BATCH else b + CTX_OFFSET)
                    mm = product(G(n), WH[:, WKV2, 0, cols], WL[:, WKV2, 0, cols],
                                 WH[:, 0, CTX_SLICE, :], WL[:, 0, CTX_SLICE, :], True, True)
                else:
                    m = (WK if is_k else WQ) if layer == SELF else WQ2
                    for k in range(KT):
                        mm = product(G(n), WH[:, m, k, cols], WL[:, m, k, cols], xTH[:, k, :], xTL[:, k, :],
                                     k == 0, k == KT - 1)
                mm.then_inc(g_full, 1)

            def project_V(b, t, layer):
                n = use_V(b, t)
                take_bank(n)
                rows = slice(t * P, (t + 1) * P)
                if layer == SELF:
                    for k in range(KT):
                        mm = product(G(n), xTH[:, k, rows], xTL[:, k, rows], WH[:, WV, k, :], WL[:, WV, k, :],
                                     k == 0, k == KT - 1)
                else:
                    mm = product(G(n), WH[:, 0, CTX_SLICE, rows], WL[:, 0, CTX_SLICE, rows],
                                 WH[:, WKV2, 1, :], WL[:, WKV2, 1, :], True, True)
                mm.then_inc(g_full, 1)

            def project_out(b, t, layer):
                n = use_Wo(b, t)
                take_bank(n)
                if t == 0:
                    pe.wait_ge(oL_done, units(b, GROUPS))
                rows = slice(t * P, (t + 1) * P)
                m = WO if layer == SELF else WO2
                for g in range(GROUPS):
                    mm = product(G(n), oTH[:, g, rows], oTL[:, g, rows], WH[:, m, g, :], WL[:, m, g, :],
                                 g == 0, g == GROUPS - 1)
                mm.then_inc(g_full, 1)

            def scores_for_max(b, g, h, q, layer):
                par = g % 2
                if h == 0 and q == 0:
                    pe.wait_ge(stack_in[par], b * (2 * STACKED) + STACKED * (g // 2 + 1))
                if not (isinstance(b, int) and b == 0 and g == 0 and h == 0 and q < 2):
                    pe.wait_ge(s_done, b * 64 + (16 * g + 4 * h + q - 1))
                n = keys(layer, q)
                dst = PS[:, S_BANK + q % 2, :]
                mm = nc.tensor.matmul(dst[:, 0:n], stackQ[0:STACK, par, h, q * P:(q + 1) * P],
                                      stackK[0:STACK, par, h, 0:n], start=True, stop=layer == SELF)
                if layer == CROSS:
                    mm = nc.tensor.matmul(dst[:, n - P:n], identb[:, :], mask_qk[:, :], start=False, stop=True)
                mm.then_inc(s_full, 1)

            def scores(b, g, k, h, layer):
                par = g % 2
                if k == 0 and h == 0:
                    pe.wait_ge(m_in[par], b * (2 * MAXED) + MAXED * (g // 2 + 1))
                if not (isinstance(b, int) and b == 0 and g == 0 and k == 0 and h < 2):
                    pe.wait_ge(p_ready, b * 64 + (16 * g + 4 * k + h - 1))
                q0 = queries(layer, k)
                dst = PS[:, T_BANK + h % 2, :]
                mm = nc.tensor.matmul(dst[:, q0:SEQ], stackK[0:STACK + 2, par, h, k * P:(k + 1) * P],
                                      stackQ[0:STACK + 2, par, h, q0:SEQ], start=True, stop=layer == SELF)
                if layer == CROSS:
                    mm = nc.tensor.matmul(dst[:, q0:q0 + P], identb[:, :], mask_kq[:, :], start=False, stop=True)
                mm.then_inc(t_full, 1)

            def transpose_max(b, g):
                n = use_m(b, g)
                take_bank(n)
                pe.wait_ge(s_done, b * 64 + 16 * (g + 1))
                nc.tensor.transpose(G(n)[0:HPG * KT, 0:P], m_cols[:, :], ident[:, :]).then_inc(g_full, 1)

            def weigh_values(b, g, k, layer):
                if g == 0:
                    pe.wait_ge(g_done, use(*use_V(b, k)) + 1)
                if k == 0 and not (isinstance(b, int) and b == 0 and g == 0):
                    pe.wait_ge(o_done, units(b, g))
                pe.wait_ge(p_ready, b * 64 + (16 * g + 4 * k + 4))
                q0 = queries(layer, k)
                for dst in (O_BANK, R_BANK):
                    for h in range(HPG):
                        lhs = V[:, k, (g * HPG + h) * HEAD:(g * HPG + h + 1) * HEAD] if dst == O_BANK else ones[:, :]
                        mm = nc.tensor.matmul(PS[h * HEAD:(h + 1) * HEAD, dst, q0:SEQ], lhs,
                                              PT[:, (4 * k + h) % 8, q0:SEQ], start=k == 0, stop=k == KT - 1)
                mm.then_inc(p_used, 1)

            pe.wait_ge(consts, 12)
            for t in range(KT):
                transpose_x(0, t)
            pe.wait_ge(w_ready, KT)
            project_QK(0, 0, False, SELF)
            pe.wait_ge(w_ready, 2 * KT)
            project_QK(0, 0, True, SELF)
            project_QK(0, 1, False, SELF)
            for h in range(HPG):
                for q in range(KT):
                    scores_for_max(0, 0, h, q, SELF)
            transpose_max(0, 0)
            project_QK(0, 1, True, SELF)
            pe.wait_ge(w_ready, 3 * KT)
            project_V(0, 0, SELF)
            project_V(0, 1, SELF)

            def slot(b, g, layer, after):
                b1_, g1 = following(b, g, 1)
                b2_, g2 = following(b, g, 2)
                layer1 = layer if g < 3 else after
                layer2 = layer if g < 2 else after
                for k in range(KT):
                    for i in range(4):
                        scores(b, g, k, i, layer)
                        if layer1 is not None:
                            scores_for_max(b1_, g1, k, i, layer1)
                    if k >= 1:
                        weigh_values(b, g, k - 1, layer)
                    if g == 0:
                        if k < 2:
                            project_V(b, 2 + k, layer)
                        if not (isinstance(b, int) and b == 0):
                            before = SELF if isinstance(b, int) and b == BATCH else layer
                            for t in ((), (0,), (1,), (2, 3))[k]:
                                project_out(b - 1, t, before)
                    if g == 2 and after is not None:
                        transpose_x(b + 1, k)
                if isinstance(b, int) and b == 0 and g == 0:
                    pe.wait_ge(w_ready, 4 * KT)
                if layer2 is not None:
                    if layer2 != layer and g == 2:
                        pe.wait_ge(raw_split, KT)
                    project_QK(b2_, g2, False, layer2)
                if layer1 is not None:
                    transpose_max(b1_, g1)
                weigh_values(b, g, KT - 1, layer)
                if layer2 is not None:
                    project_QK(b2_, g2, True, layer2)
                if g == 3 and after is not None:
                    for t in range(2):
                        project_V(b + 1, t, after)

            batches(pe, slot)

            def transpose_f(b, t):
                if not (isinstance(b, int) and b == 0 and t < 2):
                    pe.wait_ge(f_done, b * KT + (t - 1))
                pe.wait_ge(xn_done, b * KT + (2 * BATCH * KT + t + 1))
                for k in range(KT):
                    mm = nc.tensor.transpose(F(t)[:, k * P:(k + 1) * P], xn[:, t % 2, k * P:(k + 1) * P], ident[:, :])
                mm.then_inc(f_full, 1)

            def up(b, i):
                j = CHUNK_ORDER[i]
                if i == 0:
                    pe.wait_ge(f_done, b * KT + KT)
                if not (isinstance(b, int) and b == 0 and i < 2):
                    pe.wait_ge(h_gelu, b * CHUNKS + (i - 1))
                for k in range(KT):
                    cols = slice(k * P, (k + 1) * P)
                    mm = product(PS[:, H_BANK + i % 2, :], FH[:, j, cols], FL[:, j, cols], fTH[:, k, :], fTL[:, k, :],
                                 k == 0, k == KT - 1)
                mm.then_inc(h_full, 1)

            def down(b, i):
                j = CHUNK_ORDER[i]
                pe.wait_ge(h_ready, b * CHUNKS + (i + 1))
                if i == 0 and not (isinstance(b, int) and b == 0):
                    pe.wait_ge(y_done, b * KT)
                for t in range(KT):
                    rows = slice(t * P, (t + 1) * P)
                    mm = product(PS[:, ACC_BANK + t, :], hidH[:, i % 2, rows], hidL[:, i % 2, rows],
                                 FH[:, j, DIM:CHUNK], FL[:, j, DIM:CHUNK], i == 0, i == CHUNKS - 1)
                mm.then_inc(h_used, 1)

            for t in range(KT):
                project_out(2 * BATCH - 1, t, CROSS)
            pe.wait_ge(g_done, use(2 * BATCH, 5) + 1)
            for t in range(KT):
                transpose_f(0, t)

            def ffn_batch(b, first, last):
                for i in range(CHUNKS):
                    if first:
                        if i < EARLY:
                            pe.wait_ge(raw_split, RAW_TOTAL - EARLY + i + 1)
                        else:
                            pe.wait_ge(fw_ready, i + 1 - EARLY)
                    up(b, i)
                    if i == CHUNKS - 1 and not last:
                        transpose_f(b + 1, 0)
                        transpose_f(b + 1, 1)
                    if i:
                        down(b, i - 1)
                if not last:
                    transpose_f(b + 1, 2)
                    transpose_f(b + 1, 3)
                down(b, CHUNKS - 1)

            ffn_batch(0, True, False)
            with pe.Fori(1, BATCH - 1) as b:
                ffn_batch(b, False, False)
            ffn_batch(BATCH - 1, False, True)

        @block.vector
        def _(dve):
            def low_weight(m, buf, k):
                dve.wait_ge(wH_ready, m * KT + k + 1)
                nc.vector.tensor_tensor(WL[:, m, k, :], buf[:, k, :], WH[:, m, k, :].bitcast(F32),
                                        ALU.subtract).then_inc(w_ready, 1)

            def row_of(b, layer):
                return b * KT + (0 if layer == SELF else -BATCH * KT)

            def norm_stats(b, first_row):
                for t in range(KT):
                    nc.vector.bn_stats(stats[:, t, :], residual(first_row + t)).then_inc(stats_done, 1)
                dve.wait_ge(stats_done, b * KT + KT)
                nc.vector.memset(spare[:, :], 0.0).then_inc(spare_done, 1)
                for t in range(KT):
                    nc.vector.bn_aggr(mv[:, t, :], stats[:, t, :]).then_inc(mv_done, 1)

            def normed(b, t, first_row):
                if t == 0:
                    dve.wait_ge(rstd_done, b + 1)
                nc.vector.tensor_scalar(xn[:, t % 2, :], residual(first_row + t), mv[:, t, 0:1], rstd[:, t:t + 1],
                                        ALU.subtract, ALU.mult).then_inc(xn_done, 1)

            def low_xT(b, t):
                n = use_xT(b, t)
                dve.wait_ge(g_high, high_count(*n))
                nc.vector.tensor_tensor(xTL[:, :, t * P:(t + 1) * P], G(n).rearrange("p (k n) -> p k n", k=KT),
                                        xTH[:, :, t * P:(t + 1) * P].bitcast(F32), ALU.subtract).then_inc(g_done, 1)

            def low_QK(b, g, is_k, layer):
                n = (use_K if is_k else use_Q)(b, g)
                dve.wait_ge(g_high, high_count(*n))
                if layer == SELF:
                    nc.vector.scalar_tensor_tensor(out=stL[:, :], in0=G(n), scalar=(bkc if is_k else bqc)[:, g:g + 1],
                                                   in1=stH[:, :].bitcast(F32), op0=ALU.add,
                                                   op1=ALU.subtract).then_inc(g_done, 1)
                else:
                    nc.vector.tensor_tensor(stL[:, :], G(n), stH[:, :].bitcast(F32), ALU.subtract).then_inc(g_done, 1)

            def take_V(b, t, layer):
                n = use_V(b, t)
                dve.wait_ge(g_full, use(*n) + 1)
                if layer == SELF:
                    nc.vector.tensor_tensor(V[:, t, :], G(n), bv_b[:, :], ALU.add).then_inc(g_done, 1)
                else:
                    nc.vector.tensor_copy(V[:, t, :], G(n)).then_inc(g_done, 1)

            def add_residual(b, t, layer):
                n = use_Wo(b, t)
                dve.wait_ge(g_full, use(*n) + 1)
                if layer == SELF:
                    dve.wait_ge(bo_added, b * KT + (t + 1))
                tile = residual(row_of(b, layer) + t)
                nc.vector.tensor_tensor(tile, tile, G(n), ALU.add).then_inc(g_done, 1)

            def maximum(b, g, h, q, layer):
                dve.wait_ge(s_full, b * 64 + (16 * g + 4 * h + q + 1))
                nc.vector.tensor_reduce(m_cols[:, h * KT + q:h * KT + q + 1],
                                        PS[:, S_BANK + q % 2, 0:keys(layer, q)], AX.X, ALU.max).then_inc(s_done, 1)

            def take_max(b, g):
                n = use_m(b, g)
                dve.wait_ge(g_full, use(*n) + 1)
                if not (isinstance(b, int) and b == 0 and g == 0):
                    pb, pg = preceding(b, g)
                    dve.wait_ge(m_in[pg % 2], pb * (2 * MAXED) + MAXED * (pg // 2 + 1))
                rows = G(n)[0:HPG * KT, 0:P]
                nc.vector.tensor_scalar(m_row[:, 0, :], rows, -1.0, None, ALU.mult).then_inc(m_high, 1)
                dve.wait_ge(m_high, units(b, g) + 1)
                nc.vector.scalar_tensor_tensor(out=m_row[:, 1, :], in0=rows, scalar=-1.0,
                                               in1=m_row[:, 0, :].bitcast(F32), op0=ALU.mult,
                                               op1=ALU.subtract).then_inc(g_done, 1)

            def divide(b, g):
                dve.wait_ge(p_used, b * 16 + (4 * g + 4))
                if not (isinstance(b, int) and b == 0 and g == 0):
                    dve.wait_ge(oL_done, units(b, g))
                nc.vector.reciprocal(oT[:, :], PS[:, R_BANK, :]).then_inc(r_done, 1)
                dve.wait_ge(r_done, units(b, g) + 1)
                nc.vector.tensor_tensor(oT[:, :], PS[:, O_BANK, :], oT[:, :], ALU.mult).then_inc(o_done, 1)

            dve.wait_ge(x_loaded, DMA)
            norm_stats(0, 0)
            for k in range(KT):
                low_weight(WQ, PT[:, 0:4, :], k)
            normed(0, 0, 0)
            normed(0, 1, 0)
            low_xT(0, 0)
            normed(0, 2, 0)
            low_xT(0, 1)
            normed(0, 3, 0)
            low_xT(0, 2)
            low_xT(0, 3)
            for k in range(KT):
                low_weight(WK, PT[:, 4:8, :], k)
            dve.wait_ge(small_loaded, DMA * SMALL)
            low_QK(0, 0, False, SELF)
            low_QK(0, 0, True, SELF)
            for k in range(KT):
                low_weight(WV, V, k)
            low_QK(0, 1, False, SELF)
            for h in range(HPG):
                for q in range(KT):
                    maximum(0, 0, h, q, SELF)
            take_max(0, 0)
            low_QK(0, 1, True, SELF)
            take_V(0, 0, SELF)
            take_V(0, 1, SELF)
            for k in range(KT):
                low_weight(WO, PT[:, 0:4, :], k)

            def slot(b, g, layer, after):
                b1_, g1 = following(b, g, 1)
                b2_, g2 = following(b, g, 2)
                layer1 = layer if g < 3 else after
                layer2 = layer if g < 2 else after
                norm_next = g == 2 and after is not None
                for k in range(KT):
                    for q in range(KT):
                        if norm_next and q == 2:
                            normed(b + 1, k, row_of(b + 1, after))
                        if layer1 is not None:
                            maximum(b1_, g1, k, q, layer1)
                    if norm_next:
                        low_xT(b + 1, k)
                    if g == 0:
                        if k < 2:
                            take_V(b, 2 + k, layer)
                        if not (isinstance(b, int) and b == 0):
                            before = SELF if isinstance(b, int) and b == BATCH else layer
                            for t in ((), (0,), (1,), (2, 3))[k]:
                                add_residual(b - 1, t, before)
                if layer2 is not None:
                    low_QK(b2_, g2, False, layer2)
                if layer1 is not None:
                    take_max(b1_, g1)
                divide(b, g)
                if layer2 is not None:
                    low_QK(b2_, g2, True, layer2)
                if g == 3 and after is not None:
                    for t in range(2):
                        take_V(b + 1, t, after)
                if g == 1:
                    if after == SELF:
                        dve.wait_ge(x_loaded, b * DMA + 2 * DMA)
                        norm_stats(b + 1, row_of(b + 1, SELF))
                    elif after == CROSS:
                        dve.wait_ge(g_done, use(b - 2, 5) + 1)
                        norm_stats(b + 1, row_of(b + 1, CROSS))

            batches(dve, slot)

            def low_chunk(i):
                dve.wait_ge(fwH_ready, i + 1 - EARLY)
                j = CHUNK_ORDER[i]
                nc.vector.tensor_tensor(FL[:, j, :], fraw(i), FH[:, j, :].bitcast(F32),
                                        ALU.subtract).then_inc(fw_ready, 1)

            def low_fT(b, t):
                dve.wait_ge(f_high, b * KT + (t + 1))
                nc.vector.tensor_tensor(fTL[:, :, t * P:(t + 1) * P], F(t).rearrange("p (k n) -> p k n", k=KT),
                                        fTH[:, :, t * P:(t + 1) * P].bitcast(F32), ALU.subtract).then_inc(f_done, 1)

            def split_hidden(b, i):
                dve.wait_ge(h_gelu, b * CHUNKS + (i + 1))
                if not (isinstance(b, int) and b == 0 and i < 2):
                    dve.wait_ge(h_used, b * CHUNKS + (i - 1))
                nc.vector.tensor_copy(hidH[:, i % 2, :], hid[:, i % 2, :]).then_inc(h_high, 1)
                dve.wait_ge(h_high, b * CHUNKS + (i + 1))
                nc.vector.tensor_tensor(hidL[:, i % 2, :], hid[:, i % 2, :], hidH[:, i % 2, :].bitcast(F32),
                                        ALU.subtract).then_inc(h_ready, 1)

            def norm_first(b):
                for t in (0, 1):
                    normed(b + 2 * BATCH, t, b * KT)

            def norm_transposed(b):
                for t in range(KT):
                    low_fT(b, t)
                    if t < 2:
                        normed(b + 2 * BATCH, t + 2, b * KT)

            def take_out(b):
                dve.wait_ge(h_used, b * CHUNKS + CHUNKS)
                for t in range(KT):
                    dve.wait_ge(b2_added, b * KT + (t + 1))
                    tile = residual(b * KT + t)
                    nc.vector.tensor_tensor(tile, tile, PS[:, ACC_BANK + t, :], ALU.add).then_inc(y_done, 1)

            for t in range(KT):
                add_residual(2 * BATCH - 1, t, CROSS)
            dve.wait_ge(g_done, use(2 * BATCH, 5) + 1)
            norm_stats(2 * BATCH, 0)
            norm_first(0)
            norm_transposed(0)

            def ffn_batch(b, first, last):
                for i in range(CHUNKS):
                    if first and i + 3 < CHUNKS:
                        low_chunk(i + 3)
                    if i == 8 and not last:
                        norm_stats(b + (2 * BATCH + 1), b * KT + KT)
                    if i == CHUNKS - 1 and not last:
                        norm_first(b + 1)
                    split_hidden(b, i)
                if not last:
                    norm_transposed(b + 1)
                take_out(b)

            ffn_batch(0, True, False)
            with dve.Fori(1, BATCH - 1) as b:
                ffn_batch(b, False, False)
            ffn_batch(BATCH - 1, False, True)


_WEIGHTS = ("L0_attn_wq", "L0_attn_wk", "L0_attn_wv", "L0_attn_wo")


def kernel(**inputs):
    import numpy as np
    import concourse.bacc as bacc
    from concourse.bass_utils import run_bass_kernel_spmd

    def rows(name):
        return np.ascontiguousarray(np.broadcast_to(np.asarray(inputs[name]), (P, DIM)))

    def columns(name):
        return np.ascontiguousarray(np.asarray(inputs[name]).reshape(-1, P).T)

    def turned(name):
        return np.ascontiguousarray(np.swapaxes(np.asarray(inputs[name]), -1, -2))

    arrays = {
        "x": np.ascontiguousarray(inputs["x"]),
        "ctxT": turned("ctx_512"),
        "wT": np.stack([np.asarray(inputs[n]).T for n in _WEIGHTS]),
        "bq": columns("L0_attn_bq"),
        "bk": columns("L0_attn_bk"),
        "bv": rows("L0_attn_bv"),
        "bo": rows("L0_attn_bo"),
        "wq2T": turned("L0_xattn_Wq"),
        "wkv2T": turned("L0_xattn_Wkv_expand"),
        "wo2T": turned("L0_xattn_Wout"),
        "p1T": turned("L0_ffn_proj1"),
        "b1": columns("L0_ffn_proj1_bias"),
        "p2T": turned("L0_ffn_proj2"),
        "b2": rows("L0_ffn_proj2_bias"),
    }
    nc = bacc.Bacc("TRN2", target_bir_lowering=False, num_devices=1)
    args = [nc.dram_tensor(n, a.shape, mybir.dt.from_np(a.dtype), kind="ExternalInput").ap() for n, a in arrays.items()]
    out = nc.dram_tensor("out", (BATCH, SEQ, DIM), F32, kind="ExternalOutput").ap()
    decoder_layer(nc, *args, out)
    r = run_bass_kernel_spmd(nc, [arrays], core_ids=[0])
    return r.results[0]["out"]
```

```python
from contextlib import ExitStack

import concourse.bass as bass
from concourse import mybir

F32 = mybir.dt.float32
F32R = mybir.dt.float32r
BF16 = mybir.dt.bfloat16
ALU = mybir.AluOpType
ACT = mybir.ActivationFunctionType
AX = mybir.AxisListType

P = 128
BATCH = 4
SEQ = 512
DIM = 512
HEAD = 32
LATENT = 128
HIDDEN = 2048
KT = DIM // P
GROUPS = 4
HPG = 4
SELF, CROSS = 0, 1
WQ, WK, WV, WO = range(4)
WKV2, WO2, WQ2 = 0, 1, 2
CTX_SLICE = 2
CHUNKS = HIDDEN // P
CHUNK = 2 * DIM
CHUNK_ORDER = [6, 7, 4, 5, 0, 1, 2, 3] + list(range(8, CHUNKS))
STACK = 3 * HEAD
SCALE = float(HEAD) ** -0.5
EPS = 1e-5
MASKED = -1e30
MAX_TILES = ((), range(0, 5), range(5, 10), range(10, 16))
OUT_TILES = ((), (), (0, 1), (2, 3))
NORM_TILES = ((), (0,), (1,), (2, 3))
EARLY = 3
SMALL = 5
DMA = 16
LAST = 2 * BATCH - 1
STACKED = 6 * DMA
MAXED = 2 * DMA


def decoder_layer(nc, x, ctxT, wT, bq, bk, bv, bo, wq2T, wkv2T, wo2T, p1T, b1, p2T, b2, out, scratch):
    x_t = x.rearrange("b (t p) n -> b p t n", p=P)
    out_t = out.rearrange("b (t p) n -> b p t n", p=P)

    ctx = ExitStack()
    with ctx:
        def sem(name):
            return ctx.enter_context(nc.semaphore(name))

        def sb(name, shape, dt, scope=ctx):
            return scope.enter_context(nc.sbuf_tensor(name, shape, dt))

        x_res = sb("x_res", [P, BATCH * KT, DIM], F32)
        xn = sb("xn", [P, 2, DIM], F32)
        raw = sb("raw", [P, CHUNK], F32)
        ident = sb("ident", [P, P], F32)
        ones = sb("ones", [P, HEAD], F32)
        identb = sb("identb", [P, P], BF16)
        mask_qk = sb("mask_qk", [P, P], BF16)
        mask_kq = sb("mask_kq", [P, P], BF16)
        stats = sb("stats", [P, KT, 6], F32)
        mv = sb("mv", [P, KT, 2], F32)
        veps = sb("veps", [P, KT], F32)
        rstd = sb("rstd", [P, KT], F32)
        mhalf = sb("mhalf", [P, KT], F32)
        spare = sb("spare", [P, 1], F32)
        epsc = sb("epsc", [P, KT], F32)
        b1c = sb("b1c", [P, CHUNKS], F32)
        bqc = sb("bqc", [P, GROUPS], F32)
        bkc = sb("bkc", [P, GROUPS], F32)
        m_cols = sb("m_cols", [P, HPG * KT], F32)

        attn = ExitStack()
        WH = sb("WH", [P, 4, KT, DIM], F32R, attn)
        stackQ = sb("stackQ", [P, 2, HPG, SEQ], F32R, attn)
        stackK = sb("stackK", [P, 2, HPG, SEQ], F32R, attn)
        WL = sb("WL", [P, 4, KT, DIM], F32R, attn)
        xTH = sb("xTH", [P, KT, SEQ], F32R, attn)
        xTL = sb("xTL", [P, KT, SEQ], F32R, attn)
        oTH = sb("oTH", [P, GROUPS, SEQ], F32R, attn)
        oTL = sb("oTL", [P, GROUPS, SEQ], F32R, attn)
        stage = sb("stage", [P, 2, SEQ], F32R, attn)
        m_row = sb("m_row", [HPG * KT, 2, P], F32R, attn)
        V = sb("V", [P, KT, DIM], F32, attn)
        PT = sb("PT", [P, 8, SEQ], F32, attn)
        oT = sb("oT", [P, SEQ], F32, attn)
        bv_b = sb("bv_b", [P, DIM], F32, attn)
        bo_b = sb("bo_b", [P, DIM], F32, attn)
        attn.close()
        ffn = ExitStack()
        FH = sb("FH", [P, CHUNKS, CHUNK], F32R, ffn)
        FL = sb("FL", [P, CHUNKS, CHUNK], F32R, ffn)
        fTH = sb("fTH", [P, KT, SEQ], F32R, ffn)
        fTL = sb("fTL", [P, KT, SEQ], F32R, ffn)
        hid = sb("hid", [P, 2, SEQ], F32, ffn)
        hidH = sb("hidH", [P, 2, SEQ], F32R, ffn)
        hidL = sb("hidL", [P, 2, SEQ], F32R, ffn)
        b2_b = sb("b2_b", [P, DIM], F32, ffn)
        raw2 = sb("raw2", [P, CHUNK], F32, ffn)
        ffn.close()

        stH, stL = stage[:, 0, :], stage[:, 1, :]
        PS = ctx.enter_context(nc.psum_tensor("PS", [P, 8, 512], F32))
        S_BANK, T_BANK, O_BANK, R_BANK, G_BANK = 0, 2, 4, 5, 6
        ACC_BANK, H_BANK = 0, 4

        x_loaded = sem("x_loaded")
        x_rest_loaded = sem("x_rest_loaded")
        stored = [sem("q_stored"), sem("k_stored")]
        small_loaded = sem("small_loaded")
        w_loaded = [sem(f"w_loaded{m}") for m in range(4)]
        consts = sem("consts")
        wH_ready = sem("wH_ready")
        w_ready = sem("w_ready")
        raw_loaded = [sem("raw_loaded0"), sem("raw_loaded1")]
        raw_high = sem("raw_high")
        raw_split = sem("raw_split")
        spare_done = sem("spare_done")
        stats_done = sem("stats_done")
        mv_done = sem("mv_done")
        veps_done = sem("veps_done")
        rstd_done = sem("rstd_done")
        xn_done = sem("xn_done")
        bo_added = sem("bo_added")
        g_full = sem("g_full")
        g_high = sem("g_high")
        g_done = sem("g_done")
        stack_in = [sem("stack_in0"), sem("stack_in1")]
        m_high = sem("m_high")
        m_in = [sem("m_in0"), sem("m_in1")]
        s_full = sem("s_full")
        s_done = sem("s_done")
        t_full = sem("t_full")
        p_ready = sem("p_ready")
        p_used = sem("p_used")
        r_done = sem("r_done")
        o_done = sem("o_done")
        oH_done = sem("oH_done")
        oL_done = sem("oL_done")
        fw_loaded = [sem("fw_loaded0"), sem("fw_loaded1")]
        fwH_ready = sem("fwH_ready")
        fw_ready = sem("fw_ready")
        f_full = sem("f_full")
        f_high = sem("f_high")
        f_done = sem("f_done")
        h_full = sem("h_full")
        h_gelu = sem("h_gelu")
        h_high = sem("h_high")
        h_ready = sem("h_ready")
        h_used = sem("h_used")
        y_done = sem("y_done")
        b2_loaded = sem("b2_loaded")
        b2_added = sem("b2_added")
        out_stored = sem("out_stored")

        def use(b, k):
            if isinstance(b, int) and b < 0:
                return {10: 0, 11: 1, 12: 2, 13: 3, 15: 4, 16: 5, 18: 6, 19: 7, 20: 8, 21: 9, 22: 10, 23: 11}[k]
            if isinstance(b, int) and b == 0 and k < 3:
                return 12 + k
            if isinstance(b, int) and b == LAST and k > 9:
                return LAST * 24 + 8 + {14: 10, 17: 11}[k]
            if isinstance(b, int) and b > LAST:
                return LAST * 24 + 8 + 12 + (k - 3)
            return b * 24 + (8 + k)

        def bank(k, b):
            return G_BANK + (use(b, k) if isinstance(b, int) else 8 + k) % 2

        def use_xT(b, t):
            return b - 1, 10 + t

        def use_Q(b, g):
            return [(b - 1, 15), (b - 1, 18), (b - 1, 21), (b, 8)][g]

        def use_K(b, g):
            return [(b - 1, 16), (b - 1, 19), (b, 0), (b, 9)][g]

        def use_m(b, g):
            return [(b - 1, 20), (b, 7), (b, 14), (b, 17)][g]

        def use_V(b, t):
            return [(b - 1, 22), (b - 1, 23), (b, 1), (b, 2)][t]

        def use_Wo(b, t):
            return b + 1, 3 + t

        def units(b, g):
            return b * GROUPS + g

        def high_count(b, k):
            return b * 12 + (9 + {0: 1, 8: 2, 9: 3, 10: 4, 11: 5, 12: 6, 13: 7, 15: 8, 16: 9, 18: 10, 19: 11, 21: 12}[k])

        def G(n):
            return PS[:, bank(n[1], n[0]), :]

        def F(t):
            return PS[:, G_BANK + t % 2, :]

        def residual(row):
            return x_res[:, bass.ds(row, 1), :].rearrange("p o n -> p (o n)")

        def fraw(i):
            return (raw, raw2)[i % 2][:, :]

        def preceding(b, g):
            return (b, g - 1) if g else (b - 1, GROUPS - 1)

        def following(b, g, d):
            return (b, g + d) if g + d < GROUPS else (b + 1, g + d - GROUPS)

        def batches(eng, slot):
            slot(0, 0, SELF, SELF)
            with eng.Fori(0, BATCH - 1) as b:
                for g in range(1, GROUPS):
                    slot(b, g, SELF, SELF)
                slot(b + 1, 0, SELF, SELF)
            for g in range(1, GROUPS):
                slot(BATCH - 1, g, SELF, CROSS)
            slot(BATCH, 0, CROSS, CROSS)
            with eng.Fori(BATCH, 2 * BATCH - 1) as b:
                for g in range(1, GROUPS):
                    slot(b, g, CROSS, CROSS)
                slot(b + 1, 0, CROSS, CROSS)
            for g in range(1, GROUPS):
                slot(2 * BATCH - 1, g, CROSS, None)

        def queries(layer, k):
            return k * P if layer == CROSS else 0

        def keys(layer, q):
            return (q + 1) * P if layer == CROSS else SEQ

        def half(n):
            return raw[:, n % 2 * DIM:n % 2 * DIM + DIM]

        RAW = []
        for k in range(KT):
            RAW.append(((BATCH - 1, 1), [(half(k), wq2T[k * P:(k + 1) * P, :])],
                        WH[:, WQ2, k, :], WL[:, WQ2, k, :], use(*use_V(BATCH - 1, 3)) + 1))
        for k in range(2):
            RAW.append(((BATCH - 1, 1), [(half(k), wkv2T[:, k * DIM:(k + 1) * DIM])],
                        WH[:, WKV2, k, :], WL[:, WKV2, k, :], use(*use_Q(BATCH - 1, 3)) + 1))
        RAW.append(((BATCH - 1, 1), [(half(0), ctxT[0, :, 0:SEQ])],
                    WH[:, 0, CTX_SLICE, :], WL[:, 0, CTX_SLICE, :], use(*use_Q(BATCH - 1, 3)) + 1))
        FIRST_CTX = len(RAW)
        for k in range(KT):
            RAW.append(((BATCH - 1, 2), [(half(k + 1), wo2T[k * P:(k + 1) * P, :])],
                        WH[:, WO2, k, :], WL[:, WO2, k, :], use(*use_K(BATCH - 1, 3)) + 1))
        CTX_FROM = len(RAW)
        CTX_OFFSET = CTX_FROM - BATCH

        def raws_of(b, g, layer, after):
            found = [(n if n < CTX_FROM else n + BATCH - 1, src, high, low, free)
                     for n, (at, src, high, low, free) in enumerate(RAW)
                     if isinstance(b, int) and at == (b, g)]
            if g == 1 and layer == CROSS and after == CROSS:
                src = ctxT[bass.ds(b + (1 - BATCH), 1), :, 0:SEQ].rearrange("o p n -> (o p) n")
                found = [(b + CTX_OFFSET, [(half(0), src)], WH[:, 0, CTX_SLICE, :], WL[:, 0, CTX_SLICE, :],
                          use(*use_K(b, GROUPS - 1)) + 1)]
            return found

        def chunk_loads(i, buf):
            j = CHUNK_ORDER[i]
            return [(buf[:, 0:DIM].rearrange("p (k n) -> p k n", k=KT),
                     p1T.rearrange("(k p) n -> p k n", p=P)[:, :, j * P:(j + 1) * P]),
                    (buf[:, DIM:CHUNK], p2T[j * P:(j + 1) * P, :])]

        for i in range(EARLY):
            free = use(*use_Wo(BATCH - 1, 3)) if i < 2 else use(*use_Q(LAST, 3))
            RAW.append(((2 * BATCH - 1, 1 + i), chunk_loads(i, raw),
                        FH[:, CHUNK_ORDER[i], :], FL[:, CHUNK_ORDER[i], :], free + 1))
        RAW_TOTAL = len(RAW) + BATCH - 1

        def raw_arrival(n):
            if not isinstance(n, int):
                return raw_loaded[0], n * DMA + (-CTX_FROM + (CTX_FROM + 1) // 2 + 1) * DMA
            if n < CTX_FROM:
                return raw_loaded[n % 2], (n // 2 + 1) * DMA
            chunk = n - (RAW_TOTAL - EARLY)
            return raw_loaded[0], ((CTX_FROM + 1) // 2 + BATCH - 1 + 2 * (chunk + 1)) * DMA

        block = ctx.enter_context(nc.Block())

        @block.sync
        def _(sp):
            sp.dma_start(x_res[:, 0:KT, :], x_t[0]).then_inc(x_loaded, DMA)
            for m, buf in ((WQ, PT[:, 0:4, :]), (WK, PT[:, 4:8, :]), (WV, V[:, :, :])):
                sp.dma_start(buf, wT[m].rearrange("(k p) n -> p k n", p=P)).then_inc(w_loaded[m], DMA)
            sp.wait_ge(w_ready, KT)
            sp.dma_start(PT[:, 0:4, :], wT[WO].rearrange("(k p) n -> p k n", p=P)).then_inc(w_loaded[WO], DMA)

            sp.dma_start(x_res[:, KT:BATCH * KT, :].rearrange("p (b t) n -> p b t n", b=BATCH - 1),
                         x.rearrange("b (t p) n -> p b t n", p=P)[:, 1:BATCH]).then_inc(x_rest_loaded, DMA)

            def store_parts(b, g, is_k):
                sp.wait_ge(g_done, use(*(use_K if is_k else use_Q)(b, g)) + 1)
                sp.dma_start(scratch[int(is_k), g % 2], stage[:, :, :].bitcast(F32)).then_inc(stored[int(is_k)], DMA)

            def load_stacks(b, g):
                par = g % 2
                if not (isinstance(b, int) and b == 0 and g < 2):
                    sp.wait_ge(t_full, b * 64 + 16 * (g - 1))
                for is_k, stack in ((0, stackQ), (1, stackK)):
                    if is_k:
                        sp.wait_ge(stored[1], b * (GROUPS * DMA) + (g + 1) * DMA)
                    parts = scratch[is_k, par].rearrange("(h r) s n -> s r h n", h=HPG)
                    pair, single = (HEAD, 0) if is_k else (0, 2 * HEAD)
                    for s_ in range(2):
                        sp.dma_start(stack[pair + s_ * HEAD:pair + (s_ + 1) * HEAD, par, :, :].bitcast(F32),
                                     parts[s_]).then_inc(stack_in[par], DMA)
                    sp.dma_start(stack[single:single + HEAD, par, :, :].bitcast(F32), parts[0]).then_inc(stack_in[par], DMA)

            def store_max(b, g):
                par = g % 2
                sp.wait_ge(g_done, use(*use_m(b, g)) + 1)
                for j in range(2):
                    sp.dma_start(stackQ[STACK + j:STACK + j + 1, par, :, :].bitcast(F32).rearrange("o h n -> o (h n)"),
                                 m_row[:, j, :].bitcast(F32)).then_inc(m_in[par], DMA)

            for g in range(2):
                store_parts(0, g, False)
                store_parts(0, g, True)
                load_stacks(0, g)
            store_max(0, 0)
            store_parts(0, 2, False)

            def slot(b, g, layer, after):
                if g < 2 or after is not None:
                    store_parts(*following(b, g, 2), True)
                    load_stacks(*following(b, g, 2))
                if g < 3 or after is not None:
                    store_max(*following(b, g, 1))
                if g < 1 or after is not None:
                    store_parts(*following(b, g, 3), False)

            batches(sp, slot)

            sp.wait_ge(f_full, 1)
            sp.dma_start(b2_b[:, :], b2).then_inc(b2_loaded, DMA)
            for i in range(EARLY, CHUNKS):
                if i == EARLY + 1:
                    sp.wait_ge(raw_split, RAW_TOTAL)
                elif i > EARLY + 1:
                    sp.wait_ge(fw_ready, i - 1 - EARLY)
                for dst, src in chunk_loads(i, fraw(i)):
                    sp.dma_start(dst, src).then_inc(fw_loaded[i % 2], DMA)

            with sp.Fori(0, BATCH) as b:
                sp.wait_ge(y_done, b * KT + KT)
                sp.dma_start(out_t[bass.ds(b, 1)].rearrange("o p t n -> (o p) t n"),
                             x_res[:, bass.ds(b * KT, KT), :]).then_inc(out_stored, DMA)
            sp.wait_ge(out_stored, DMA * BATCH)

        @block.gpsimd
        def _(pool):
            pool.memset(ident[:, :], 0.0).then_inc(consts, 1)
            pool.memset(identb[:, :], 0.0).then_inc(consts, 1)
            pool.memset(mask_qk[:, :], 0.0).then_inc(consts, 1)
            pool.memset(mask_kq[:, :], 0.0).then_inc(consts, 1)
            pool.memset(mhalf[:, :], -0.5).then_inc(consts, 1)
            pool.memset(epsc[:, :], EPS).then_inc(consts, 1)
            pool.memset(ones[:, :], 1.0).then_inc(consts, 1)
            pool.wait_ge(consts, 7)
            pool.memset(stackK[STACK:STACK + 2, :, :, :].bitcast(F32), 1.0).then_inc(consts, 1)
            pool.wait_ge(consts, 8)
            for t in (ident, identb):
                pool.affine_select(out=t[:, :], in_=t[:, :], compare_op=ALU.not_equal, fill=1.0,
                                   base=0, pattern=[[-1, P]], channel_multiplier=1).then_inc(consts, 1)
            pool.affine_select(out=mask_qk[:, :], in_=mask_qk[:, :], compare_op=ALU.is_ge, fill=MASKED,
                               base=0, pattern=[[-1, P]], channel_multiplier=1).then_inc(consts, 1)
            pool.affine_select(out=mask_kq[:, :], in_=mask_kq[:, :], compare_op=ALU.is_ge, fill=MASKED,
                               base=0, pattern=[[1, P]], channel_multiplier=-1).then_inc(consts, 1)

            def root(b):
                pool.wait_ge(mv_done, b * KT + KT)
                pool.tensor_tensor(veps[:, :], mv[:, :, 1], epsc[:, :], ALU.add).then_inc(veps_done, 1)
                pool.wait_ge(veps_done, b + 1)
                pool.tensor_tensor(rstd[:, :], veps[:, :], mhalf[:, :], ALU.pow).then_inc(rstd_done, 1)

            def add_bo(b):
                for t in range(KT):
                    pool.wait_ge(xn_done, b * KT + (t + 1))
                    tile = residual(b * KT + t)
                    pool.tensor_tensor(tile, tile, bo_b[:, :], ALU.add).then_inc(bo_added, 1)

            def pass_raws(raws):
                ahead = 2 if len(raws) > 1 else 1

                def load(n, src, *_):
                    if not (isinstance(n, int) and n < ahead):
                        pool.wait_ge(raw_split, n - (ahead - 1))
                    for dst, part in src:
                        pool.dma_start(dst, part).then_inc(raw_loaded[n % 2 if ahead == 2 else 0], DMA)

                for r in raws[:ahead]:
                    load(*r)
                for i, (n, src, high, low, _) in enumerate(raws):
                    pool.wait_ge(raw_high, n + 1)
                    pool.tensor_tensor(low, src[0][0] if len(src) == 1 else raw[:, :], high.bitcast(F32),
                                       ALU.subtract).then_inc(raw_split, 1)
                    if i + ahead < len(raws):
                        load(*raws[i + ahead])

            def low_output(b, g):
                pool.wait_ge(oH_done, units(b, g) + 1)
                pool.tensor_tensor(oTL[:, g, :], oT[:, :], oTH[:, g, :].bitcast(F32),
                                   ALU.subtract).then_inc(oL_done, 1)

            root(0)
            pool.wait_ge(small_loaded, DMA * SMALL)
            add_bo(0)

            def slot(b, g, layer, after):
                if g == 1 and after is not None:
                    root(b + 1)
                if not (isinstance(b, int) and b == 0 and g == 0):
                    low_output(*preceding(b, g))
                if g == 2 and after == SELF:
                    add_bo(b + 1)
                raws = raws_of(b, g, layer, after)
                if raws:
                    pass_raws(raws)

            batches(pool, slot)
            low_output(2 * BATCH - 1, GROUPS - 1)

            def ffn_norm(b):
                root(b + 2 * BATCH)
                for t in range(KT):
                    pool.wait_ge(xn_done, b * KT + (2 * BATCH * KT + t + 1))
                    tile = residual(b * KT + t)
                    pool.tensor_tensor(tile, tile, b2_b[:, :], ALU.add).then_inc(b2_added, 1)

            root(2 * BATCH)
            pool.wait_ge(b2_loaded, DMA)
            for t in range(KT):
                pool.wait_ge(xn_done, 2 * BATCH * KT + t + 1)
                pool.tensor_tensor(x_res[:, t, :], x_res[:, t, :], b2_b[:, :], ALU.add).then_inc(b2_added, 1)
            with pool.Fori(1, BATCH) as b:
                ffn_norm(b)

        @block.scalar
        def _(act):
            for dst, src in ((bqc[:, :], bq), (bkc[:, :], bk), (bv_b[:, :], bv), (bo_b[:, :], bo), (b1c[:, :], b1)):
                act.dma_start(dst, src).then_inc(small_loaded, DMA)

            def high_weight(m, buf):
                act.wait_ge(w_loaded[m], DMA)
                for k in range(KT):
                    nc.scalar.activation(WH[:, m, k, :], buf[:, k, :], ACT.Copy).then_inc(wH_ready, 1)

            def high_xT(b, t):
                n = use_xT(b, t)
                act.wait_ge(g_full, use(*n) + 1)
                nc.scalar.activation(xTH[:, :, t * P:(t + 1) * P],
                                     G(n).rearrange("p (k n) -> p k n", k=KT), ACT.Copy).then_inc(g_high, 1)

            def high_QK(b, g, is_k, layer):
                n = (use_K if is_k else use_Q)(b, g)
                act.wait_ge(g_full, use(*n) + 1)
                if is_k:
                    act.wait_ge(stored[0], b * (GROUPS * DMA) + (g + 1) * DMA)
                elif not (isinstance(b, int) and b == 0 and g == 0):
                    act.wait_ge(stored[1], b * (GROUPS * DMA) + g * DMA)
                if layer == SELF:
                    nc.scalar.activation(stH, G(n), ACT.Identity,
                                         bias=(bkc if is_k else bqc)[:, g:g + 1]).then_inc(g_high, 1)
                else:
                    nc.scalar.activation(stH, G(n), ACT.Copy).then_inc(g_high, 1)

            def high_output(b, g):
                act.wait_ge(o_done, units(b, g) + 1)
                if g == 0:
                    act.wait_ge(g_full, b * 24 + (8 + 7))
                nc.scalar.activation(oTH[:, g, :], oT[:, :], ACT.Copy).then_inc(oH_done, 1)

            def high_raw(n, src, high, _, free):
                act.wait_ge(g_full, free)
                act.wait_ge(*raw_arrival(n))
                nc.scalar.activation(high, src[0][0] if len(src) == 1 else raw[:, :], ACT.Copy).then_inc(raw_high, 1)

            high_weight(WQ, PT[:, 0:4, :])
            for t in range(KT):
                high_xT(0, t)
            high_weight(WK, PT[:, 4:8, :])
            act.wait_ge(small_loaded, DMA * SMALL)
            high_QK(0, 0, False, SELF)
            high_QK(0, 0, True, SELF)
            high_QK(0, 1, False, SELF)
            high_QK(0, 1, True, SELF)
            high_weight(WV, V)
            high_QK(0, 2, False, SELF)
            high_weight(WO, PT[:, 0:4, :])
            act.wait_ge(w_ready, 4 * KT)

            def slot(b, g, layer, after):
                raws = raws_of(b, g, layer, after)
                shares = [[], raws[0:2], raws[2:4], raws[4:]] if len(raws) > 3 else [[], raws, [], []]
                for k in range(KT):
                    if not (isinstance(b, int) and b == 0 and g == 0 and k < 2):
                        act.wait_ge(p_used, b * 16 + (4 * g + k - 1))
                    for h in range(HPG):
                        act.wait_ge(t_full, b * 64 + (16 * g + 4 * k + h + 1))
                        q0 = queries(layer, k)
                        nc.scalar.activation(PT[:, (4 * k + h) % 8, q0:SEQ], PS[:, T_BANK + h % 2, q0:SEQ],
                                             ACT.Exp, scale=SCALE).then_inc(p_ready, 1)
                    if k == 0:
                        if g < 2 or after is not None:
                            high_QK(*following(b, g, 2), True, layer if g < 2 else after)
                        if not (isinstance(b, int) and b == 0 and g == 0):
                            high_output(*preceding(b, g))
                    if g == 1 and after is not None:
                        for t in NORM_TILES[k]:
                            high_xT(b + 1, t)
                    for r in shares[k]:
                        high_raw(*r)
                if g < 1 or after is not None:
                    high_QK(*following(b, g, 3), False, layer if g < 1 else after)

            batches(act, slot)
            high_output(2 * BATCH - 1, GROUPS - 1)

            def high_fT(b, t):
                act.wait_ge(f_full, b * KT + (t + 1))
                nc.scalar.activation(fTH[:, :, t * P:(t + 1) * P],
                                     F(t).rearrange("p (k n) -> p k n", k=KT), ACT.Copy).then_inc(f_high, 1)

            def gelu(b, i):
                act.wait_ge(h_full, b * CHUNKS + (i + 1))
                if not (isinstance(b, int) and b == 0 and i < 2):
                    act.wait_ge(h_ready, b * CHUNKS + (i - 1))
                j = CHUNK_ORDER[i]
                nc.scalar.activation(hid[:, i % 2, :], PS[:, H_BANK + i % 2, :], ACT.Gelu,
                                     bias=b1c[:, j:j + 1]).then_inc(h_gelu, 1)

            def high_chunk(i):
                act.wait_ge(fw_loaded[i % 2], DMA * 2 * ((i - EARLY) // 2 + 1))
                nc.scalar.activation(FH[:, CHUNK_ORDER[i], :], fraw(i), ACT.Copy).then_inc(fwH_ready, 1)

            for t in range(KT):
                high_fT(0, t)
            for i in range(CHUNKS):
                if i + 3 < CHUNKS:
                    high_chunk(i + 3)
                gelu(0, i)
            for t in range(KT):
                high_fT(1, t)
            with act.Fori(1, BATCH - 1) as b:
                for i in range(CHUNKS):
                    gelu(b, i)
                for t in range(KT):
                    high_fT(b + 1, t)
            for i in range(CHUNKS):
                gelu(BATCH - 1, i)

        @block.tensor
        def _(pe):
            def product(dst, wH, wL, mH, mL, first, last):
                nc.tensor.matmul(dst, wH, mH, start=first, stop=False)
                nc.tensor.matmul(dst, wH, mL, start=False, stop=False)
                return nc.tensor.matmul(dst, wL, mH, start=False, stop=last)

            def take_bank(n):
                if not (isinstance(n[0], int) and use(*n) < 2):
                    pe.wait_ge(g_done, use(*n) - 1)

            def transpose_x(b, t):
                n = use_xT(b, t)
                take_bank(n)
                pe.wait_ge(xn_done, b * KT + (t + 1))
                for k in range(KT):
                    mm = nc.tensor.transpose(G(n)[:, k * P:(k + 1) * P], xn[:, t % 2, k * P:(k + 1) * P], ident[:, :])
                mm.then_inc(g_full, 1)

            def project_QK(b, g, is_k, layer):
                n = (use_K if is_k else use_Q)(b, g)
                take_bank(n)
                if g == 0:
                    pe.wait_ge(g_done, use(*use_xT(b, KT - 1)) + 1)
                cols = slice(g * P, (g + 1) * P)
                if layer == CROSS and is_k:
                    if g == 0:
                        pe.wait_ge(raw_split, FIRST_CTX if isinstance(b, int) and b == BATCH else b + CTX_OFFSET)
                    mm = product(G(n), WH[:, WKV2, 0, cols], WL[:, WKV2, 0, cols],
                                 WH[:, 0, CTX_SLICE, :], WL[:, 0, CTX_SLICE, :], True, True)
                else:
                    m = (WK if is_k else WQ) if layer == SELF else WQ2
                    for k in range(KT):
                        mm = product(G(n), WH[:, m, k, cols], WL[:, m, k, cols], xTH[:, k, :], xTL[:, k, :],
                                     k == 0, k == KT - 1)
                mm.then_inc(g_full, 1)

            def project_V(b, t, layer):
                n = use_V(b, t)
                take_bank(n)
                rows = slice(t * P, (t + 1) * P)
                if layer == SELF:
                    for k in range(KT):
                        mm = product(G(n), xTH[:, k, rows], xTL[:, k, rows], WH[:, WV, k, :], WL[:, WV, k, :],
                                     k == 0, k == KT - 1)
                else:
                    mm = product(G(n), WH[:, 0, CTX_SLICE, rows], WL[:, 0, CTX_SLICE, rows],
                                 WH[:, WKV2, 1, :], WL[:, WKV2, 1, :], True, True)
                mm.then_inc(g_full, 1)

            def project_out(b, t, layer):
                n = use_Wo(b, t)
                take_bank(n)
                if t == 0:
                    pe.wait_ge(oL_done, units(b, GROUPS))
                rows = slice(t * P, (t + 1) * P)
                m = WO if layer == SELF else WO2
                for g in range(GROUPS):
                    mm = product(G(n), oTH[:, g, rows], oTL[:, g, rows], WH[:, m, g, :], WL[:, m, g, :],
                                 g == 0, g == GROUPS - 1)
                mm.then_inc(g_full, 1)

            def scores_for_max(b, g, h, q, layer):
                par = g % 2
                if h == 0 and q == 0:
                    pe.wait_ge(stack_in[par], b * (2 * STACKED) + STACKED * (g // 2 + 1))
                if not (isinstance(b, int) and b == 0 and g == 0 and h == 0 and q < 2):
                    pe.wait_ge(s_done, b * 64 + (16 * g + 4 * h + q - 1))
                n = keys(layer, q)
                dst = PS[:, S_BANK + q % 2, :]
                mm = nc.tensor.matmul(dst[:, 0:n], stackQ[0:STACK, par, h, q * P:(q + 1) * P],
                                      stackK[0:STACK, par, h, 0:n], start=True, stop=layer == SELF)
                if layer == CROSS:
                    mm = nc.tensor.matmul(dst[:, n - P:n], identb[:, :], mask_qk[:, :], start=False, stop=True)
                mm.then_inc(s_full, 1)

            def scores(b, g, k, h, layer):
                par = g % 2
                if k == 0 and h == 0:
                    pe.wait_ge(m_in[par], b * (2 * MAXED) + MAXED * (g // 2 + 1))
                if not (isinstance(b, int) and b == 0 and g == 0 and k == 0 and h < 2):
                    pe.wait_ge(p_ready, b * 64 + (16 * g + 4 * k + h - 1))
                q0 = queries(layer, k)
                dst = PS[:, T_BANK + h % 2, :]
                mm = nc.tensor.matmul(dst[:, q0:SEQ], stackK[0:STACK + 2, par, h, k * P:(k + 1) * P],
                                      stackQ[0:STACK + 2, par, h, q0:SEQ], start=True, stop=layer == SELF)
                if layer == CROSS:
                    mm = nc.tensor.matmul(dst[:, q0:q0 + P], identb[:, :], mask_kq[:, :], start=False, stop=True)
                mm.then_inc(t_full, 1)

            def transpose_max(b, g):
                n = use_m(b, g)
                take_bank(n)
                pe.wait_ge(s_done, b * 64 + 16 * (g + 1))
                nc.tensor.transpose(G(n)[0:HPG * KT, 0:P], m_cols[:, :], ident[:, :]).then_inc(g_full, 1)

            def weigh_values(b, g, k, layer):
                if g == 0:
                    pe.wait_ge(g_done, use(*use_V(b, k)) + 1)
                if k == 0 and not (isinstance(b, int) and b == 0 and g == 0):
                    pe.wait_ge(o_done, units(b, g))
                pe.wait_ge(p_ready, b * 64 + (16 * g + 4 * k + 4))
                q0 = queries(layer, k)
                for dst in (O_BANK, R_BANK):
                    for h in range(HPG):
                        lhs = V[:, k, (g * HPG + h) * HEAD:(g * HPG + h + 1) * HEAD] if dst == O_BANK else ones[:, :]
                        mm = nc.tensor.matmul(PS[h * HEAD:(h + 1) * HEAD, dst, q0:SEQ], lhs,
                                              PT[:, (4 * k + h) % 8, q0:SEQ], start=k == 0, stop=k == KT - 1)
                mm.then_inc(p_used, 1)

            pe.wait_ge(consts, 12)
            for t in range(KT):
                transpose_x(0, t)
            pe.wait_ge(w_ready, KT)
            project_QK(0, 0, False, SELF)
            pe.wait_ge(w_ready, 2 * KT)
            project_QK(0, 0, True, SELF)
            project_QK(0, 1, False, SELF)
            project_QK(0, 1, True, SELF)
            for h in range(HPG):
                for q in range(KT):
                    scores_for_max(0, 0, h, q, SELF)
            transpose_max(0, 0)
            project_QK(0, 2, False, SELF)
            pe.wait_ge(w_ready, 3 * KT)
            project_V(0, 0, SELF)
            project_V(0, 1, SELF)

            def slot(b, g, layer, after):
                b1_, g1 = following(b, g, 1)
                layer1 = layer if g < 3 else after
                layer2 = layer if g < 2 else after
                layer3 = layer if g < 1 else after
                for k in range(KT):
                    tiles = list(MAX_TILES[k]) if layer1 is not None else []
                    for i in range(HPG):
                        scores(b, g, k, i, layer)
                        for n in tiles[i:i + 1] if i < HPG - 1 else tiles[i:]:
                            scores_for_max(b1_, g1, n // KT, n % KT, layer1)
                    if k == 0 and layer2 is not None:
                        project_QK(*following(b, g, 2), True, layer2)
                    if k >= 1:
                        weigh_values(b, g, k - 1, layer)
                    if g == 0:
                        if k < 2:
                            project_V(b, 2 + k, layer)
                        if not (isinstance(b, int) and b == 0):
                            before = SELF if isinstance(b, int) and b == BATCH else layer
                            for t in OUT_TILES[k]:
                                project_out(b - 1, t, before)
                    if g == 1 and after is not None:
                        for t in NORM_TILES[k]:
                            transpose_x(b + 1, t)
                if isinstance(b, int) and b == 0 and g == 0:
                    pe.wait_ge(w_ready, 4 * KT)
                if layer1 is not None:
                    transpose_max(b1_, g1)
                weigh_values(b, g, KT - 1, layer)
                if layer3 is not None:
                    if layer3 != layer and g == 1:
                        pe.wait_ge(raw_split, KT)
                    project_QK(*following(b, g, 3), False, layer3)
                if g == 3 and after is not None:
                    for t in range(2):
                        project_V(b + 1, t, after)

            batches(pe, slot)

            def transpose_f(b, t):
                if not (isinstance(b, int) and b == 0 and t < 2):
                    pe.wait_ge(f_done, b * KT + (t - 1))
                pe.wait_ge(xn_done, b * KT + (2 * BATCH * KT + t + 1))
                for k in range(KT):
                    mm = nc.tensor.transpose(F(t)[:, k * P:(k + 1) * P], xn[:, t % 2, k * P:(k + 1) * P], ident[:, :])
                mm.then_inc(f_full, 1)

            def up(b, i):
                j = CHUNK_ORDER[i]
                if i == 0:
                    pe.wait_ge(f_done, b * KT + KT)
                if not (isinstance(b, int) and b == 0 and i < 2):
                    pe.wait_ge(h_gelu, b * CHUNKS + (i - 1))
                for k in range(KT):
                    cols = slice(k * P, (k + 1) * P)
                    mm = product(PS[:, H_BANK + i % 2, :], FH[:, j, cols], FL[:, j, cols], fTH[:, k, :], fTL[:, k, :],
                                 k == 0, k == KT - 1)
                mm.then_inc(h_full, 1)

            def down(b, i):
                j = CHUNK_ORDER[i]
                pe.wait_ge(h_ready, b * CHUNKS + (i + 1))
                if i == 0 and not (isinstance(b, int) and b == 0):
                    pe.wait_ge(y_done, b * KT)
                for t in range(KT):
                    rows = slice(t * P, (t + 1) * P)
                    mm = product(PS[:, ACC_BANK + t, :], hidH[:, i % 2, rows], hidL[:, i % 2, rows],
                                 FH[:, j, DIM:CHUNK], FL[:, j, DIM:CHUNK], i == 0, i == CHUNKS - 1)
                mm.then_inc(h_used, 1)

            for t in range(KT):
                project_out(2 * BATCH - 1, t, CROSS)
            pe.wait_ge(g_done, use(*use_Wo(LAST, KT - 1)) + 1)
            for t in range(KT):
                transpose_f(0, t)

            def ffn_batch(b, first, last):
                for i in range(CHUNKS):
                    if first:
                        if i < EARLY:
                            pe.wait_ge(raw_split, RAW_TOTAL - EARLY + i + 1)
                        else:
                            pe.wait_ge(fw_ready, i + 1 - EARLY)
                    up(b, i)
                    if i == CHUNKS - 1 and not last:
                        transpose_f(b + 1, 0)
                        transpose_f(b + 1, 1)
                    if i:
                        down(b, i - 1)
                if not last:
                    transpose_f(b + 1, 2)
                    transpose_f(b + 1, 3)
                down(b, CHUNKS - 1)

            ffn_batch(0, True, False)
            with pe.Fori(1, BATCH - 1) as b:
                ffn_batch(b, False, False)
            ffn_batch(BATCH - 1, False, True)

        @block.vector
        def _(dve):
            def low_weight(m, buf, k):
                dve.wait_ge(wH_ready, m * KT + k + 1)
                nc.vector.tensor_tensor(WL[:, m, k, :], buf[:, k, :], WH[:, m, k, :].bitcast(F32),
                                        ALU.subtract).then_inc(w_ready, 1)

            def row_of(b, layer):
                return b * KT + (0 if layer == SELF else -BATCH * KT)

            def norm_stats(b, first_row):
                for t in range(KT):
                    nc.vector.bn_stats(stats[:, t, :], residual(first_row + t)).then_inc(stats_done, 1)
                dve.wait_ge(stats_done, b * KT + KT)
                nc.vector.memset(spare[:, :], 0.0).then_inc(spare_done, 1)
                for t in range(KT):
                    nc.vector.bn_aggr(mv[:, t, :], stats[:, t, :]).then_inc(mv_done, 1)

            def normed(b, t, first_row):
                if t == 0:
                    dve.wait_ge(rstd_done, b + 1)
                nc.vector.tensor_scalar(xn[:, t % 2, :], residual(first_row + t), mv[:, t, 0:1], rstd[:, t:t + 1],
                                        ALU.subtract, ALU.mult).then_inc(xn_done, 1)

            def low_xT(b, t):
                n = use_xT(b, t)
                dve.wait_ge(g_high, high_count(*n))
                nc.vector.tensor_tensor(xTL[:, :, t * P:(t + 1) * P], G(n).rearrange("p (k n) -> p k n", k=KT),
                                        xTH[:, :, t * P:(t + 1) * P].bitcast(F32), ALU.subtract).then_inc(g_done, 1)

            def low_QK(b, g, is_k, layer):
                n = (use_K if is_k else use_Q)(b, g)
                dve.wait_ge(g_high, high_count(*n))
                if layer == SELF:
                    nc.vector.scalar_tensor_tensor(out=stL, in0=G(n), scalar=(bkc if is_k else bqc)[:, g:g + 1],
                                                   in1=stH.bitcast(F32), op0=ALU.add,
                                                   op1=ALU.subtract).then_inc(g_done, 1)
                else:
                    nc.vector.tensor_tensor(stL, G(n), stH.bitcast(F32), ALU.subtract).then_inc(g_done, 1)

            def take_V(b, t, layer):
                n = use_V(b, t)
                dve.wait_ge(g_full, use(*n) + 1)
                if layer == SELF:
                    nc.vector.tensor_tensor(V[:, t, :], G(n), bv_b[:, :], ALU.add).then_inc(g_done, 1)
                else:
                    nc.vector.tensor_copy(V[:, t, :], G(n)).then_inc(g_done, 1)

            def add_residual(b, t, layer):
                n = use_Wo(b, t)
                dve.wait_ge(g_full, use(*n) + 1)
                if layer == SELF:
                    dve.wait_ge(bo_added, b * KT + (t + 1))
                tile = residual(row_of(b, layer) + t)
                nc.vector.tensor_tensor(tile, tile, G(n), ALU.add).then_inc(g_done, 1)

            def maximum(b, g, h, q, layer):
                dve.wait_ge(s_full, b * 64 + (16 * g + 4 * h + q + 1))
                nc.vector.tensor_reduce(m_cols[:, h * KT + q:h * KT + q + 1],
                                        PS[:, S_BANK + q % 2, 0:keys(layer, q)], AX.X, ALU.max).then_inc(s_done, 1)

            def take_max(b, g):
                n = use_m(b, g)
                dve.wait_ge(g_full, use(*n) + 1)
                if not (isinstance(b, int) and b == 0 and g == 0):
                    pb, pg = preceding(b, g)
                    dve.wait_ge(m_in[pg % 2], pb * (2 * MAXED) + MAXED * (pg // 2 + 1))
                rows = G(n)[0:HPG * KT, 0:P]
                nc.vector.tensor_scalar(m_row[:, 0, :], rows, -1.0, None, ALU.mult).then_inc(m_high, 1)
                dve.wait_ge(m_high, units(b, g) + 1)
                nc.vector.scalar_tensor_tensor(out=m_row[:, 1, :], in0=rows, scalar=-1.0,
                                               in1=m_row[:, 0, :].bitcast(F32), op0=ALU.mult,
                                               op1=ALU.subtract).then_inc(g_done, 1)

            def divide(b, g):
                dve.wait_ge(p_used, b * 16 + (4 * g + 4))
                if not (isinstance(b, int) and b == 0 and g == 0):
                    dve.wait_ge(oL_done, units(b, g))
                nc.vector.reciprocal(oT[:, :], PS[:, R_BANK, :]).then_inc(r_done, 1)
                dve.wait_ge(r_done, units(b, g) + 1)
                nc.vector.tensor_tensor(oT[:, :], PS[:, O_BANK, :], oT[:, :], ALU.mult).then_inc(o_done, 1)

            dve.wait_ge(x_loaded, DMA)
            norm_stats(0, 0)
            for k in range(KT):
                low_weight(WQ, PT[:, 0:4, :], k)
            normed(0, 0, 0)
            normed(0, 1, 0)
            low_xT(0, 0)
            normed(0, 2, 0)
            low_xT(0, 1)
            normed(0, 3, 0)
            low_xT(0, 2)
            low_xT(0, 3)
            for k in range(KT):
                low_weight(WK, PT[:, 4:8, :], k)
            dve.wait_ge(small_loaded, DMA * SMALL)
            low_QK(0, 0, False, SELF)
            low_QK(0, 0, True, SELF)
            low_QK(0, 1, False, SELF)
            low_QK(0, 1, True, SELF)
            for k in range(KT):
                low_weight(WV, V, k)
            for h in range(HPG):
                for q in range(KT):
                    maximum(0, 0, h, q, SELF)
            take_max(0, 0)
            low_QK(0, 2, False, SELF)
            take_V(0, 0, SELF)
            take_V(0, 1, SELF)
            for k in range(KT):
                low_weight(WO, PT[:, 0:4, :], k)

            def slot(b, g, layer, after):
                b1_, g1 = following(b, g, 1)
                layer1 = layer if g < 3 else after
                layer2 = layer if g < 2 else after
                layer3 = layer if g < 1 else after
                norm_next = g == 1 and after is not None
                for k in range(KT):
                    if k == 0:
                        if layer2 is not None:
                            low_QK(*following(b, g, 2), True, layer2)
                        if norm_next:
                            if after == SELF:
                                dve.wait_ge(x_rest_loaded, DMA)
                            else:
                                dve.wait_ge(g_done, use(*use_Wo(b - (BATCH - 1), KT - 1)) + 1)
                            norm_stats(b + 1, row_of(b + 1, after))
                    if layer1 is not None:
                        for n in MAX_TILES[k]:
                            maximum(b1_, g1, n // KT, n % KT, layer1)
                            if norm_next and n == 2:
                                normed(b + 1, 0, row_of(b + 1, after))
                                normed(b + 1, 1, row_of(b + 1, after))
                    if norm_next:
                        for t in NORM_TILES[k]:
                            low_xT(b + 1, t)
                            if t < 2:
                                normed(b + 1, t + 2, row_of(b + 1, after))
                    if g == 0:
                        if k < 2:
                            take_V(b, 2 + k, layer)
                        if not (isinstance(b, int) and b == 0):
                            before = SELF if isinstance(b, int) and b == BATCH else layer
                            for t in OUT_TILES[k]:
                                add_residual(b - 1, t, before)
                if layer1 is not None:
                    take_max(b1_, g1)
                divide(b, g)
                if layer3 is not None:
                    low_QK(*following(b, g, 3), False, layer3)
                if g == 3 and after is not None:
                    for t in range(2):
                        take_V(b + 1, t, after)

            batches(dve, slot)

            def low_chunk(i):
                dve.wait_ge(fwH_ready, i + 1 - EARLY)
                j = CHUNK_ORDER[i]
                nc.vector.tensor_tensor(FL[:, j, :], fraw(i), FH[:, j, :].bitcast(F32),
                                        ALU.subtract).then_inc(fw_ready, 1)

            def low_fT(b, t):
                dve.wait_ge(f_high, b * KT + (t + 1))
                nc.vector.tensor_tensor(fTL[:, :, t * P:(t + 1) * P], F(t).rearrange("p (k n) -> p k n", k=KT),
                                        fTH[:, :, t * P:(t + 1) * P].bitcast(F32), ALU.subtract).then_inc(f_done, 1)

            def split_hidden(b, i):
                dve.wait_ge(h_gelu, b * CHUNKS + (i + 1))
                if not (isinstance(b, int) and b == 0 and i < 2):
                    dve.wait_ge(h_used, b * CHUNKS + (i - 1))
                nc.vector.tensor_copy(hidH[:, i % 2, :], hid[:, i % 2, :]).then_inc(h_high, 1)
                dve.wait_ge(h_high, b * CHUNKS + (i + 1))
                nc.vector.tensor_tensor(hidL[:, i % 2, :], hid[:, i % 2, :], hidH[:, i % 2, :].bitcast(F32),
                                        ALU.subtract).then_inc(h_ready, 1)

            def norm_first(b):
                for t in (0, 1):
                    normed(b + 2 * BATCH, t, b * KT)

            def norm_transposed(b):
                for t in range(KT):
                    low_fT(b, t)
                    if t < 2:
                        normed(b + 2 * BATCH, t + 2, b * KT)

            def take_out(b):
                dve.wait_ge(h_used, b * CHUNKS + CHUNKS)
                for t in range(KT):
                    dve.wait_ge(b2_added, b * KT + (t + 1))
                    tile = residual(b * KT + t)
                    nc.vector.tensor_tensor(tile, tile, PS[:, ACC_BANK + t, :], ALU.add).then_inc(y_done, 1)

            for t in range(KT):
                add_residual(2 * BATCH - 1, t, CROSS)
            dve.wait_ge(g_done, use(*use_Wo(LAST, KT - 1)) + 1)
            norm_stats(2 * BATCH, 0)
            norm_first(0)
            norm_transposed(0)

            def ffn_batch(b, first, last):
                for i in range(CHUNKS):
                    if first and i + 3 < CHUNKS:
                        low_chunk(i + 3)
                    if i == 8 and not last:
                        norm_stats(b + (2 * BATCH + 1), b * KT + KT)
                    if i == CHUNKS - 1 and not last:
                        norm_first(b + 1)
                    split_hidden(b, i)
                if not last:
                    norm_transposed(b + 1)
                take_out(b)

            ffn_batch(0, True, False)
            with dve.Fori(1, BATCH - 1) as b:
                ffn_batch(b, False, False)
            ffn_batch(BATCH - 1, False, True)


_WEIGHTS = ("L0_attn_wq", "L0_attn_wk", "L0_attn_wv", "L0_attn_wo")


def kernel(**inputs):
    import numpy as np
    import concourse.bacc as bacc
    from concourse.bass_utils import run_bass_kernel_spmd

    def rows(name):
        return np.ascontiguousarray(np.broadcast_to(np.asarray(inputs[name]), (P, DIM)))

    def columns(name):
        return np.ascontiguousarray(np.asarray(inputs[name]).reshape(-1, P).T)

    def turned(name):
        return np.ascontiguousarray(np.swapaxes(np.asarray(inputs[name]), -1, -2))

    arrays = {
        "x": np.ascontiguousarray(inputs["x"]),
        "ctxT": turned("ctx_512"),
        "wT": np.stack([np.asarray(inputs[n]).T for n in _WEIGHTS]),
        "bq": columns("L0_attn_bq"),
        "bk": columns("L0_attn_bk"),
        "bv": rows("L0_attn_bv"),
        "bo": rows("L0_attn_bo"),
        "wq2T": turned("L0_xattn_Wq"),
        "wkv2T": turned("L0_xattn_Wkv_expand"),
        "wo2T": turned("L0_xattn_Wout"),
        "p1T": turned("L0_ffn_proj1"),
        "b1": columns("L0_ffn_proj1_bias"),
        "p2T": turned("L0_ffn_proj2"),
        "b2": rows("L0_ffn_proj2_bias"),
    }
    nc = bacc.Bacc("TRN2", target_bir_lowering=False, num_devices=1)
    args = [nc.dram_tensor(n, a.shape, mybir.dt.from_np(a.dtype), kind="ExternalInput").ap() for n, a in arrays.items()]
    out = nc.dram_tensor("out", (BATCH, SEQ, DIM), F32, kind="ExternalOutput").ap()
    scratch = nc.dram_tensor("scratch", (2, 2, P, 2, SEQ), F32, kind="Internal").ap()
    decoder_layer(nc, *args, out, scratch)
    r = run_bass_kernel_spmd(nc, [arrays], core_ids=[0])
    return r.results[0]["out"]
```

```python
from contextlib import ExitStack

import concourse.bass as bass
from concourse import mybir

F32 = mybir.dt.float32
F32R = mybir.dt.float32r
BF16 = mybir.dt.bfloat16
ALU = mybir.AluOpType
ACT = mybir.ActivationFunctionType
AX = mybir.AxisListType

P = 128
BATCH = 4
SEQ = 512
DIM = 512
HEAD = 32
LATENT = 128
HIDDEN = 2048
KT = DIM // P
GROUPS = 4
HPG = 4
SELF, CROSS, FFN = 0, 1, 2
WQ, WK, WV, WO = range(4)
WKV2, WO2, WQ2 = 0, 1, 2
CTX_SLICE = 2
CHUNKS = HIDDEN // P
CHUNK = 2 * DIM
CHUNK_ORDER = [6, 7, 4, 5, 0, 1, 2, 3] + list(range(8, CHUNKS))
STACK = 3 * HEAD
SCALE = float(HEAD) ** -0.5
EPS = 1e-5
MASKED = -1e30
PLACES = {
    SELF: dict(
        scores=((0.0, 0.045), (0.015, 0.042), (-0.05, 0.042), (-0.031, 0.041)),
        max=((0.036, 0.043), (0.03, 0.042), (0.03, 0.042), (0.062, 0.042)),
        turn_max=(0.8, 0.797, 0.72, 0.72),
        values_after=0.112, add_after=0.03, sums_after=(0.082, 0.153), divide=0.81, output=0.157, lag=0.04,
        K=((-0.032, 0.16), (0.0, 0.22), (0.051, 0.4), (0.014, 0.2)),
        Q=((0.84, 0.995), (0.968, 0.969), (0.84, 0.969), (0.84, 0.969)),
        V_here=((0.16, 0.25), (0.25, 0.363)), V_next=((0.25, 0.342), (0.452, 0.606)),
        out=(0.341, 0.78),
        stats=(0.087, 0.25, 0.439, 0.545), aggregate=0.65, normed=(0.9, 0.95),
        norm=(0.292, 0.46, 0.52, 0.607), bias=(0.033, 0.05, 0.847, 0.9),
        raw=(0.303, 0.088)),
    CROSS: dict(
        scores=((-0.043, 0.044), (-0.033, 0.038), (-0.05, 0.039), (0.0, 0.038)),
        max=((0.03, 0.042), (0.035, 0.042), (0.03, 0.042), (0.03, 0.042)),
        turn_max=(0.8, 0.72, 0.72, 0.72),
        values_after=0.08, add_after=0.03, sums_after=(0.1, 0.184), divide=0.81, output=0.122, lag=0.04,
        K=((0.0, 0.171), (0.0, 0.236), (0.047, 0.4), (0.0, 0.2)),
        Q=((0.84, 0.969), (0.917, 1.021), (0.84, 0.969), (0.84, 0.969)),
        V_here=((0.16, 0.25), (0.25, 0.34)), V_next=((0.208, 0.45), (0.45, 0.655)),
        out=(0.36, 0.76),
        stats=(0.1, 0.218, 0.4, 0.493), aggregate=0.65, normed=(0.879, 0.95),
        norm=(0.28, 0.4, 0.52, 0.64), bias=(0.0, 0.05, 0.819, 0.947),
        raw=(0.312, 0.09)),
}
UP_AT = ((0.752, 1.0), (0.056, 0.412))
CHUNK_AT = (0.335, 0.5)
EARLY = 6
FIRST_UPS = 4
CHUNKS_AHEAD = EARLY - FIRST_UPS
SMALL = 5
DMA = 16
LAST = 2 * BATCH - 1
STACKED = 4 * DMA
STORED = 2 * DMA
MAXED = 2 * DMA
ADDS = 2 * HPG


def decoder_layer(nc, x, ctxT, wT, bq, bk, bv, bo, wq2T, wkv2T, wo2T, p1T, b1, p2T, b2, out, scratch):
    x_t = x.rearrange("b (t p) n -> b p t n", p=P)
    out_t = out.rearrange("b (t p) n -> b p t n", p=P)

    ctx = ExitStack()
    with ctx:
        def sem(name):
            return ctx.enter_context(nc.semaphore(name))

        def sb(name, shape, dt, scope=ctx):
            return scope.enter_context(nc.sbuf_tensor(name, shape, dt))

        x_res = sb("x_res", [P, BATCH * KT, DIM], F32)
        xn = sb("xn", [P, 2, DIM], F32)
        xTH = sb("xTH", [P, KT, SEQ], F32R)
        xTL = sb("xTL", [P, KT, SEQ], F32R)
        raw = sb("raw", [P, CHUNK], F32)
        ident = sb("ident", [P, P], F32)
        ones = sb("ones", [P, HEAD], F32)
        identb = sb("identb", [P, P], BF16)
        mask_qk = sb("mask_qk", [P, P], BF16)
        mask_kq = sb("mask_kq", [P, P], BF16)
        stats = sb("stats", [P, KT, 6], F32)
        mv = sb("mv", [P, KT, 2], F32)
        veps = sb("veps", [P, KT], F32)
        rstd = sb("rstd", [P, KT], F32)
        mhalf = sb("mhalf", [P, KT], F32)
        spare = sb("spare", [P, 1], F32)
        epsc = sb("epsc", [P, KT], F32)
        b1c = sb("b1c", [P, CHUNKS], F32)
        bqc = sb("bqc", [P, GROUPS], F32)
        bkc = sb("bkc", [P, GROUPS], F32)
        m_cols = sb("m_cols", [P, HPG * KT], F32)

        attn = ExitStack()
        WH = sb("WH", [P, 4, KT, DIM], F32R, attn)
        stackQ = sb("stackQ", [P, 2, HPG, SEQ], F32R, attn)
        stackK = sb("stackK", [P, 2, HPG, SEQ], F32R, attn)
        WL = sb("WL", [P, 4, KT, DIM], F32R, attn)
        PT = sb("PT", [P, 8, SEQ], F32, attn)
        oTH = sb("oTH", [P, GROUPS, SEQ], F32R, attn)
        oTL = sb("oTL", [P, GROUPS, SEQ], F32R, attn)
        stage = sb("stage", [P, 2, SEQ], F32R, attn)
        m_row = sb("m_row", [HPG * KT, 2, P], F32R, attn)
        V = sb("V", [P, KT, DIM], F32, attn)
        P_sum = sb("P_sum", [P, HPG, SEQ], F32, attn)
        attn.close()
        ffn = ExitStack()
        FH = sb("FH", [P, CHUNKS, CHUNK], F32R, ffn)
        FL = sb("FL", [P, CHUNKS, CHUNK], F32R, ffn)
        hid = sb("hid", [P, 2, SEQ], F32, ffn)
        hidH = sb("hidH", [P, 2, SEQ], F32R, ffn)
        hidL = sb("hidL", [P, 2, SEQ], F32R, ffn)
        b2_b = sb("b2_b", [P, DIM], F32, ffn)
        raw2 = sb("raw2", [P, CHUNK], F32, ffn)
        ffn.close()

        oT = P_sum[:, HPG - 1, :]
        bv_b, bo_b = raw[:, 0:DIM], raw[:, DIM:CHUNK]
        stH, stL = stage[:, 0, :], stage[:, 1, :]
        PS = ctx.enter_context(nc.psum_tensor("PS", [P, 8, 512], F32))
        S_BANK, T_BANK, O_BANK, R_BANK, G_BANK = 0, 2, 4, 5, 6
        ACC_BANK, H_BANK = 0, 4

        x_loaded = sem("x_loaded")
        x_rest_loaded = sem("x_rest_loaded")
        stored = [sem("q_stored"), sem("k_stored")]
        small_loaded = sem("small_loaded")
        w_loaded = [sem(f"w_loaded{m}") for m in range(4)]
        consts = sem("consts")
        wH_ready = sem("wH_ready")
        w_ready = sem("w_ready")
        raw_loaded = [sem("raw_loaded0"), sem("raw_loaded1")]
        raw_high = sem("raw_high")
        raw_split = sem("raw_split")
        spare_done = sem("spare_done")
        stats_done = sem("stats_done")
        mv_done = sem("mv_done")
        veps_done = sem("veps_done")
        rstd_done = sem("rstd_done")
        xn_done = sem("xn_done")
        bo_added = sem("bo_added")
        g_full = sem("g_full")
        g_high = sem("g_high")
        g_done = sem("g_done")
        stack_in = [sem("stack_in0"), sem("stack_in1")]
        m_high = sem("m_high")
        m_in = [sem("m_in0"), sem("m_in1")]
        s_full = sem("s_full")
        s_done = sem("s_done")
        t_full = sem("t_full")
        p_ready = sem("p_ready")
        p_used = sem("p_used")
        p_added = sem("p_added")
        zeroed = sem("zeroed")
        r_done = sem("r_done")
        o_done = sem("o_done")
        oH_done = sem("oH_done")
        oL_done = sem("oL_done")
        fw_loaded = [sem("fw_loaded0"), sem("fw_loaded1")]
        fwH_ready = sem("fwH_ready")
        fw_ready = sem("fw_ready")
        f_full = sem("f_full")
        f_high = sem("f_high")
        f_done = sem("f_done")
        h_full = sem("h_full")
        h_gelu = sem("h_gelu")
        h_high = sem("h_high")
        h_ready = sem("h_ready")
        h_used = sem("h_used")
        y_done = sem("y_done")
        b2_loaded = sem("b2_loaded")
        b2_added = sem("b2_added")
        out_stored = sem("out_stored")

        def use(b, k):
            if isinstance(b, int) and b < 0:
                return {10: 0, 11: 1, 12: 2, 13: 3, 15: 4, 16: 5, 20: 6, 21: 7, 18: 8, 19: 9, 22: 10, 23: 11}[k]
            if isinstance(b, int) and b == 0 and k < 3:
                return 12 + k
            if isinstance(b, int) and b == LAST and k > 9:
                return LAST * 24 + 8 + {10: 10, 11: 11, 12: 12, 13: 13, 14: 14, 17: 15}[k]
            if isinstance(b, int) and b > LAST:
                return LAST * 24 + 8 + 16 + (k - 3)
            return b * 24 + (8 + k)

        def bank(k, b):
            return G_BANK + (use(b, k) if isinstance(b, int) else 8 + k) % 2

        def use_xT(b, t):
            return b - 1, 10 + t

        def use_Q(b, g):
            return [(b - 1, 15), (b - 1, 18), (b - 1, 23), (b, 8)][g]

        def use_K(b, g):
            return [(b - 1, 16), (b - 1, 19), (b, 0), (b, 9)][g]

        def use_m(b, g):
            return [(b - 1, 22), (b, 7), (b, 14), (b, 17)][g]

        def use_V(b, t):
            return [(b - 1, 20), (b - 1, 21), (b, 1), (b, 2)][t]

        def use_Wo(b, t):
            return b + 1, 3 + t

        def units(b, g):
            return b * GROUPS + g

        def high_count(b, k):
            return b * 12 + (9 + {0: 1, 8: 2, 9: 3, 10: 4, 11: 5, 12: 6, 13: 7, 15: 8, 16: 9, 18: 10, 19: 11, 23: 12}[k])

        def G(n):
            return PS[:, bank(n[1], n[0]), :]

        def F(t):
            return PS[:, G_BANK + t % 2, :]

        def residual(row):
            return x_res[:, bass.ds(row, 1), :].rearrange("p o n -> p (o n)")

        def H(b, i):
            first = isinstance(b, int) and b == 0 and i < FIRST_UPS
            return PS[:, ACC_BANK + i if first else H_BANK + i % 2, :]

        def fraw(i):
            return (raw, raw2)[i % 2][:, :]

        def preceding(b, g):
            return (b, g - 1) if g else (b - 1, GROUPS - 1)

        def following(b, g, d):
            return (b, g + d) if g + d < GROUPS else (b + 1, g + d - GROUPS)

        def batches(eng, slot):
            def batch(b, layer, after):
                for g in range(GROUPS):
                    slot(b, g, layer, after)

            batch(0, SELF, SELF)
            with eng.Fori(1, BATCH - 1) as b:
                batch(b, SELF, SELF)
            batch(BATCH - 1, SELF, CROSS)
            batch(BATCH, CROSS, CROSS)
            with eng.Fori(BATCH + 1, LAST) as b:
                batch(b, CROSS, CROSS)
            batch(LAST, CROSS, FFN)

        def layers_ahead(g, layer, after):
            return [layer if g + d < GROUPS else after if after != FFN else None for d in (1, 2, 3)]

        def has_before(b):
            return not (isinstance(b, int) and b == 0)

        def spread(kind, window, n, tile=0):
            first, last = window
            return [(first + (last - first) * i / n, kind, tile, i) for i in range(n)]

        def tile_places(place, costs):
            first, step = place
            mean = sum(costs) / len(costs)
            return [first + step * sum(costs[:j]) / mean for j in range(len(costs))]

        def raw_place(places, after, i):
            first, step = places["raw"] if after != FFN else CHUNK_AT
            return first + i * step

        def out_place(places, t):
            first, last = places["out"]
            return first + (last - first) * t / KT

        def pe_order(b, g, layer, after):
            layer1, layer2, layer3 = layers_ahead(g, layer, after)
            places = PLACES[layer]
            scores_at = tile_places(places["scores"][g], [SEQ - queries(layer, j // HPG) + P for j in range(HPG * KT)])
            max_at = tile_places(places["max"][g], [keys(layer1, j % KT) + P for j in range(HPG * KT)])
            work = []
            for j, at in enumerate(scores_at):
                work.append((at, "scores", j // HPG, j % HPG))
                if j % HPG == HPG - 1:
                    work.append((at + places["values_after"], "values", j // HPG, 0))
                if layer1 is not None:
                    work.append((max_at[j], "max", j // KT, j % KT))
            work += [(scores_at[-1] + places["sums_after"][i], "sums", KT - 2 + i, 0) for i in range(2)]
            if layer1 is not None:
                work.append((places["turn_max"][g], "turn_max", 0, 0))
            if layer2 is not None:
                work += spread("K", places["K"][g], KT if layer2 == SELF else 1)
            if layer3 is not None:
                work += spread("Q", places["Q"][g], KT)
            if g == 0:
                for t in range(2):
                    work += spread("V", places["V_here"][t], KT if layer == SELF else 1, 2 + t)
                if has_before(b):
                    for t in range(KT):
                        work += spread("out", (out_place(places, t), out_place(places, t + 1)), GROUPS, t)
            if g == 1:
                work += [(places["norm"][t], "norm", t, 0) for t in range(KT)]
            if g >= 2 and after == FFN:
                work += spread("up", UP_AT[g - 2], KT, g - 2)
            if g == GROUPS - 1 and after != FFN:
                for t in range(2):
                    work += spread("V'", places["V_next"][t], KT if after == SELF else 1, t)
            return sorted(work, key=lambda piece: piece[0])

        def queries(layer, k):
            return k * P if layer == CROSS else 0

        def keys(layer, q):
            return (q + 1) * P if layer == CROSS else SEQ

        def half(n):
            return raw[:, n % 2 * DIM:n % 2 * DIM + DIM]

        RAW = []
        for k in range(KT):
            RAW.append(((BATCH - 1, 1), [(half(k), wq2T[k * P:(k + 1) * P, :])],
                        WH[:, WQ2, k, :], WL[:, WQ2, k, :], use(*use_V(BATCH - 1, 3)) + 1))
        for k in range(2):
            RAW.append(((BATCH - 1, 1), [(half(k), wkv2T[:, k * DIM:(k + 1) * DIM])],
                        WH[:, WKV2, k, :], WL[:, WKV2, k, :], use(*use_Q(BATCH - 1, 3)) + 1))
        RAW.append(((BATCH - 1, 1), [(half(0), ctxT[0, :, 0:SEQ])],
                    WH[:, 0, CTX_SLICE, :], WL[:, 0, CTX_SLICE, :], use(*use_Q(BATCH - 1, 3)) + 1))
        FIRST_CTX = len(RAW)
        for k in range(KT):
            RAW.append(((BATCH - 1, 3), [(half(k + 1), wo2T[k * P:(k + 1) * P, :])],
                        WH[:, WO2, k, :], WL[:, WO2, k, :], use(*use_K(BATCH - 1, 3)) + 1))
        CTX_FROM = len(RAW)
        CTX_OFFSET = CTX_FROM - BATCH

        def raws_of(b, g, layer, after):
            found = [(n if n < CTX_FROM else n + BATCH - 1, src, high, low, free)
                     for n, (at, src, high, low, free) in enumerate(RAW)
                     if isinstance(b, int) and at == (b, g)]
            if g == 1 and layer == CROSS and after == CROSS:
                src = ctxT[bass.ds(b + (1 - BATCH), 1), :, 0:SEQ].rearrange("o p n -> (o p) n")
                found = [(b + CTX_OFFSET, [(half(0), src)], WH[:, 0, CTX_SLICE, :], WL[:, 0, CTX_SLICE, :],
                          use(*use_K(b, GROUPS - 1)) + 1)]
            return found

        def chunk_loads(i, buf):
            j = CHUNK_ORDER[i]
            return [(buf[:, 0:DIM].rearrange("p (k n) -> p k n", k=KT),
                     p1T.rearrange("(k p) n -> p k n", p=P)[:, :, j * P:(j + 1) * P]),
                    (buf[:, DIM:CHUNK], p2T[j * P:(j + 1) * P, :])]

        for i in range(EARLY):
            free = use(*(use_Wo(BATCH - 1, 3), use_Q(LAST, 3), use_K(LAST, 3))[i // 2])
            RAW.append(((LAST, i // 2), chunk_loads(i, raw),
                        FH[:, CHUNK_ORDER[i], :], FL[:, CHUNK_ORDER[i], :], free + 1))
        RAW_TOTAL = len(RAW) + BATCH - 1

        def raw_arrival(n):
            if not (isinstance(n, int) and (n < CTX_FROM or n >= CTX_FROM + BATCH - 1)):
                return raw_loaded[0], n * DMA + (-CTX_FROM + (CTX_FROM + 1) // 2 + 1) * DMA
            if n < CTX_FROM:
                return raw_loaded[n % 2], (n // 2 + 1) * DMA
            chunk = n - (RAW_TOTAL - EARLY)
            return raw_loaded[0], ((CTX_FROM + 1) // 2 + BATCH - 1 + 2 * (chunk + 1)) * DMA

        block = ctx.enter_context(nc.Block())

        @block.sync
        def _(sp):
            sp.dma_start(x_res[:, 0:KT, :], x_t[0]).then_inc(x_loaded, DMA)
            for m, buf in ((WQ, PT[:, 0:4, :]), (WK, PT[:, 4:8, :]), (WV, V[:, :, :])):
                sp.dma_start(buf, wT[m].rearrange("(k p) n -> p k n", p=P)).then_inc(w_loaded[m], DMA)
            sp.wait_ge(w_ready, KT)
            sp.dma_start(PT[:, 0:4, :], wT[WO].rearrange("(k p) n -> p k n", p=P)).then_inc(w_loaded[WO], DMA)

            sp.dma_start(x_res[:, KT:BATCH * KT, :].rearrange("p (b t) n -> p b t n", b=BATCH - 1),
                         x.rearrange("b (t p) n -> p b t n", p=P)[:, 1:BATCH]).then_inc(x_rest_loaded, DMA)

            def store_parts(b, g, is_k):
                sp.wait_ge(g_done, use(*(use_K if is_k else use_Q)(b, g)) + 1)
                for part in range(2):
                    sp.dma_start(scratch[int(is_k), g % 2, part].rearrange("r h n -> h r n"),
                                 stage[:, part, :].bitcast(F32)).then_inc(stored[int(is_k)], DMA)

            def load_stacks(b, g):
                par = g % 2
                if not (isinstance(b, int) and b == 0 and g < 2):
                    sp.wait_ge(t_full, b * 64 + 16 * (g - 1))
                for is_k, stack in ((0, stackQ), (1, stackK)):
                    if is_k:
                        sp.wait_ge(stored[1], b * (GROUPS * STORED) + (g + 1) * STORED)
                    pair, single = (HEAD, 0) if is_k else (0, 2 * HEAD)
                    sp.dma_start(stack[pair:pair + 2 * HEAD, par, :, :].bitcast(F32),
                                 scratch[is_k, par].rearrange("s r h n -> (s r) h n")).then_inc(stack_in[par], DMA)
                    sp.dma_start(stack[single:single + HEAD, par, :, :].bitcast(F32),
                                 scratch[is_k, par, 0]).then_inc(stack_in[par], DMA)

            def store_max(b, g):
                par = g % 2
                sp.wait_ge(g_done, use(*use_m(b, g)) + 1)
                for j in range(2):
                    sp.dma_start(stackQ[STACK + j:STACK + j + 1, par, :, :].bitcast(F32).rearrange("o h n -> o (h n)"),
                                 m_row[:, j, :].bitcast(F32)).then_inc(m_in[par], DMA)

            for g in range(2):
                store_parts(0, g, False)
                store_parts(0, g, True)
                load_stacks(0, g)
            store_max(0, 0)
            store_parts(0, 2, False)

            def slot(b, g, layer, after):
                layer1, layer2, layer3 = layers_ahead(g, layer, after)
                if layer2 is not None:
                    store_parts(*following(b, g, 2), True)
                    load_stacks(*following(b, g, 2))
                if layer1 is not None:
                    store_max(*following(b, g, 1))
                if layer3 is not None:
                    store_parts(*following(b, g, 3), False)

            batches(sp, slot)

            sp.wait_ge(g_full, use(*use_Wo(LAST, KT - 1)) + 1)
            sp.dma_start(b2_b[:, :], b2).then_inc(b2_loaded, DMA)
            for i in range(EARLY, CHUNKS):
                if i == EARLY + 1:
                    sp.wait_ge(raw_split, RAW_TOTAL)
                elif i > EARLY + 1:
                    sp.wait_ge(fw_ready, i - 1 - EARLY)
                for dst, src in chunk_loads(i, fraw(i)):
                    sp.dma_start(dst, src).then_inc(fw_loaded[i % 2], DMA)

            with sp.Fori(0, BATCH - 1) as b:
                sp.wait_ge(y_done, b * KT + KT)
                sp.dma_start(out_t[bass.ds(b, 1)].rearrange("o p t n -> (o p) t n"),
                             x_res[:, bass.ds(b * KT, KT), :]).then_inc(out_stored, DMA)
            for t in range(KT):
                row = (BATCH - 1) * KT + t
                sp.wait_ge(y_done, row + 1)
                sp.dma_start(out_t[BATCH - 1, :, t, :], x_res[:, row, :]).then_inc(out_stored, DMA)
            sp.wait_ge(out_stored, DMA * (BATCH - 1 + KT))

        @block.gpsimd
        def _(pool):
            pool.memset(ident[:, :], 0.0).then_inc(consts, 1)
            pool.memset(identb[:, :], 0.0).then_inc(consts, 1)
            pool.memset(mask_qk[:, :], 0.0).then_inc(consts, 1)
            pool.memset(mask_kq[:, :], 0.0).then_inc(consts, 1)
            pool.memset(mhalf[:, :], -0.5).then_inc(consts, 1)
            pool.memset(epsc[:, :], EPS).then_inc(consts, 1)
            pool.memset(ones[:, :], 1.0).then_inc(consts, 1)
            pool.wait_ge(consts, 7)
            pool.memset(stackK[STACK:STACK + 2, :, :, :].bitcast(F32), 1.0).then_inc(consts, 1)
            pool.wait_ge(consts, 8)
            for t in (ident, identb):
                pool.affine_select(out=t[:, :], in_=t[:, :], compare_op=ALU.not_equal, fill=1.0,
                                   base=0, pattern=[[-1, P]], channel_multiplier=1).then_inc(consts, 1)
            pool.affine_select(out=mask_qk[:, :], in_=mask_qk[:, :], compare_op=ALU.is_ge, fill=MASKED,
                               base=0, pattern=[[-1, P]], channel_multiplier=1).then_inc(consts, 1)
            pool.affine_select(out=mask_kq[:, :], in_=mask_kq[:, :], compare_op=ALU.is_ge, fill=MASKED,
                               base=0, pattern=[[1, P]], channel_multiplier=-1).then_inc(consts, 1)

            def root(b):
                pool.wait_ge(mv_done, b * KT + KT)
                pool.tensor_tensor(veps[:, :], mv[:, :, 1], epsc[:, :], ALU.add).then_inc(veps_done, 1)
                pool.wait_ge(veps_done, b + 1)
                pool.tensor_tensor(rstd[:, :], veps[:, :], mhalf[:, :], ALU.pow).then_inc(rstd_done, 1)

            def add_bo(b, t):
                pool.wait_ge(xn_done, b * KT + (t + 1))
                tile = residual(b * KT + t)
                pool.tensor_tensor(tile, tile, bo_b, ALU.add).then_inc(bo_added, 1)

            def ahead(raws):
                return 2 if len(raws) > 1 and len(raws[0][1]) == 1 else 1

            def load_raw(raws, i):
                n, src = raws[i][:2]
                if not (isinstance(n, int) and n < ahead(raws)):
                    pool.wait_ge(raw_split, n - (ahead(raws) - 1))
                for dst, part in src:
                    pool.dma_start(dst, part).then_inc(raw_loaded[n % 2 if ahead(raws) == 2 else 0], DMA)

            def low_raw(raws, i):
                n, src, high, low, _ = raws[i]
                pool.wait_ge(raw_high, n + 1)
                pool.tensor_tensor(low, src[0][0] if len(src) == 1 else raw[:, :], high.bitcast(F32),
                                   ALU.subtract).then_inc(raw_split, 1)
                if i + ahead(raws) < len(raws):
                    load_raw(raws, i + ahead(raws))

            def low_output(b, g):
                pool.wait_ge(oH_done, units(b, g) + 1)
                pool.tensor_tensor(oTL[:, g, :], oT[:, :], oTH[:, g, :].bitcast(F32),
                                   ALU.subtract).then_inc(oL_done, 1)

            root(0)
            pool.wait_ge(small_loaded, DMA * SMALL)
            for t in range(KT):
                add_bo(0, t)

            def add_probabilities(b, g, k, h, layer):
                pool.wait_ge(p_ready, b * 64 + (16 * g + 4 * k + h + 1))
                if k == 1 and h == HPG - 1 and not (isinstance(b, int) and b == 0 and g == 0):
                    pool.wait_ge(oL_done, units(b, g))
                if k == 1:
                    pool.tensor_tensor(P_sum[:, h, :], PT[:, h, :], PT[:, 4 + h, :], ALU.add).then_inc(p_added, 1)
                else:
                    if h == 0:
                        pool.wait_ge(p_added, b * (GROUPS * ADDS) + (ADDS * g + HPG))
                    q0 = queries(layer, k)
                    pool.tensor_tensor(P_sum[:, h, q0:SEQ], P_sum[:, h, q0:SEQ], PT[:, h, q0:SEQ],
                                       ALU.add).then_inc(p_added, 1)

            def slot(b, g, layer, after):
                places = PLACES[layer]
                first = isinstance(b, int) and b == 0 and g == 0
                raws = raws_of(b, g, layer, after)
                if isinstance(b, int) and b == BATCH - 1 and g == 1:
                    pool.wait_ge(g_done, use(*use_V(BATCH - 1, KT - 1)) + 1)
                    pool.wait_ge(bo_added, BATCH * KT)
                for i in range(ahead(raws) if raws else 0):
                    load_raw(raws, i)
                if isinstance(b, int) and b == BATCH and g == 0:
                    pool.wait_ge(p_used, BATCH * GROUPS * KT)
                    pool.memset(PT[:, 4:8, 0:P], 0.0).then_inc(zeroed, 1)
                    pool.wait_ge(zeroed, 1)
                work = [(at + places["add_after"], "add", k, h) for at, kind, k, h in pe_order(b, g, layer, after)
                        if kind == "scores" and k in (1, 2)]
                if not first:
                    work.append((places["output"], "output", 0, 0))
                if g == 2 and after == SELF:
                    work += [(places["bias"][t], "bo", t, 0) for t in range(KT)]
                work += [(raw_place(places, after, i) + 0.01, "raw", i, 0) for i in range(len(raws))]
                if g == 0:
                    work.append((places["aggregate"] + 0.02, "root", 0, 0))
                for _, kind, i, h in sorted(work, key=lambda piece: piece[0]):
                    if kind == "add":
                        add_probabilities(b, g, i, h, layer)
                    elif kind == "output":
                        low_output(*preceding(b, g))
                    elif kind == "bo":
                        add_bo(b + 1, i)
                    elif kind == "raw":
                        low_raw(raws, i)
                    elif kind == "root":
                        root(b + 1)

            batches(pool, slot)
            low_output(2 * BATCH - 1, GROUPS - 1)

            def ffn_norm(b):
                root(b + 2 * BATCH)
                for t in range(KT):
                    pool.wait_ge(xn_done, b * KT + (2 * BATCH * KT + t + 1))
                    tile = residual(b * KT + t)
                    pool.tensor_tensor(tile, tile, b2_b[:, :], ALU.add).then_inc(b2_added, 1)

            pool.wait_ge(b2_loaded, DMA)
            for t in range(KT):
                pool.wait_ge(xn_done, 2 * BATCH * KT + t + 1)
                pool.tensor_tensor(x_res[:, t, :], x_res[:, t, :], b2_b[:, :], ALU.add).then_inc(b2_added, 1)
            with pool.Fori(1, BATCH) as b:
                ffn_norm(b)

        @block.scalar
        def _(act):
            for dst, src in ((bqc[:, :], bq), (bkc[:, :], bk), (bv_b, bv), (bo_b, bo), (b1c[:, :], b1)):
                act.dma_start(dst, src).then_inc(small_loaded, DMA)

            def high_weight(m, buf):
                act.wait_ge(w_loaded[m], DMA)
                for k in range(KT):
                    nc.scalar.activation(WH[:, m, k, :], buf[:, k, :], ACT.Copy).then_inc(wH_ready, 1)

            def high_xT(b, t):
                n = use_xT(b, t)
                act.wait_ge(g_full, use(*n) + 1)
                nc.scalar.activation(xTH[:, :, t * P:(t + 1) * P],
                                     G(n).rearrange("p (k n) -> p k n", k=KT), ACT.Copy).then_inc(g_high, 1)

            def high_QK(b, g, is_k, layer):
                n = (use_K if is_k else use_Q)(b, g)
                act.wait_ge(g_full, use(*n) + 1)
                if is_k:
                    act.wait_ge(stored[0], b * (GROUPS * STORED) + (g + 1) * STORED)
                elif not (isinstance(b, int) and b == 0 and g == 0):
                    act.wait_ge(stored[1], b * (GROUPS * STORED) + g * STORED)
                if layer == SELF:
                    nc.scalar.activation(stH, G(n), ACT.Identity,
                                         bias=(bkc if is_k else bqc)[:, g:g + 1]).then_inc(g_high, 1)
                else:
                    nc.scalar.activation(stH, G(n), ACT.Copy).then_inc(g_high, 1)

            def high_output(b, g):
                act.wait_ge(o_done, units(b, g) + 1)
                if g == 0:
                    act.wait_ge(g_full, b * 24 + (8 + 7))
                nc.scalar.activation(oTH[:, g, :], oT[:, :], ACT.Copy).then_inc(oH_done, 1)

            def high_raw(n, src, high, _, free):
                act.wait_ge(g_full, free)
                act.wait_ge(*raw_arrival(n))
                nc.scalar.activation(high, src[0][0] if len(src) == 1 else raw[:, :], ACT.Copy).then_inc(raw_high, 1)

            high_weight(WQ, PT[:, 0:4, :])
            for t in range(KT):
                high_xT(0, t)
            high_weight(WK, PT[:, 4:8, :])
            act.wait_ge(small_loaded, DMA * SMALL)
            high_QK(0, 0, False, SELF)
            high_weight(WV, V)
            high_QK(0, 0, True, SELF)
            high_weight(WO, PT[:, 0:4, :])
            high_QK(0, 1, False, SELF)
            high_QK(0, 1, True, SELF)
            high_QK(0, 2, False, SELF)
            act.wait_ge(w_ready, 4 * KT)

            def slot(b, g, layer, after):
                layer1, layer2, layer3 = layers_ahead(g, layer, after)
                places = PLACES[layer]
                work = [piece for piece in pe_order(b, g, layer, after) if piece[1] in ("scores", "norm")]
                if layer2 is not None:
                    work.append((places["K"][g][1], "K", 0, 0))
                if layer3 is not None:
                    work.append((places["Q"][g][1], "Q", 0, 0))
                if not (isinstance(b, int) and b == 0 and g == 0):
                    work.append((places["output"], "output", 0, 0))
                raws = raws_of(b, g, layer, after)
                work += [(raw_place(places, after, i), "raw", i, 0) for i in range(len(raws))]
                for _, kind, i, h in sorted(work, key=lambda piece: piece[0]):
                    if kind == "scores":
                        k = i
                        if h == 0 and not (isinstance(b, int) and b == 0 and g == 0 and k < 2):
                            act.wait_ge(p_used, b * 16 + (4 * g + k - 1))
                        if k == 2:
                            act.wait_ge(p_added, b * (GROUPS * ADDS) + (ADDS * g + h + 1))
                        elif k == 0 and not (isinstance(b, int) and b == 0 and g == 0):
                            act.wait_ge(p_added, b * (GROUPS * ADDS) + (ADDS * (g - 1) + HPG + h + 1))
                        act.wait_ge(t_full, b * 64 + (16 * g + 4 * k + h + 1))
                        q0 = queries(layer, k)
                        nc.scalar.activation(PT[:, (4 * k + h) % 8, q0:SEQ], PS[:, T_BANK + h % 2, q0:SEQ],
                                             ACT.Exp, scale=SCALE).then_inc(p_ready, 1)
                    elif kind == "K":
                        high_QK(*following(b, g, 2), True, layer2)
                    elif kind == "Q":
                        high_QK(*following(b, g, 3), False, layer3)
                    elif kind == "output":
                        high_output(*preceding(b, g))
                    elif kind == "norm":
                        high_xT(b + 1, i)
                    elif kind == "raw":
                        high_raw(*raws[i])

            batches(act, slot)

            def high_fT(b, t):
                act.wait_ge(f_full, b * KT + (t - (KT - 1)))
                nc.scalar.activation(xTH[:, :, t * P:(t + 1) * P],
                                     F(t).rearrange("p (k n) -> p k n", k=KT), ACT.Copy).then_inc(f_high, 1)

            def gelu(b, i):
                act.wait_ge(h_full, b * CHUNKS + (i + 1))
                if not (isinstance(b, int) and b == 0 and i < 2):
                    act.wait_ge(h_ready, b * CHUNKS + (i - 1))
                j = CHUNK_ORDER[i]
                nc.scalar.activation(hid[:, i % 2, :], H(b, i), ACT.Gelu,
                                     bias=b1c[:, j:j + 1]).then_inc(h_gelu, 1)

            def high_chunk(i):
                act.wait_ge(fw_loaded[i % 2], DMA * 2 * ((i - EARLY) // 2 + 1))
                nc.scalar.activation(FH[:, CHUNK_ORDER[i], :], fraw(i), ACT.Copy).then_inc(fwH_ready, 1)

            for i in range(CHUNKS):
                if i == 2:
                    high_output(LAST, GROUPS - 1)
                if i == FIRST_UPS:
                    act.wait_ge(g_full, use(*use_Wo(LAST, KT - 1)) + 1)
                if i >= FIRST_UPS and i + CHUNKS_AHEAD < CHUNKS:
                    high_chunk(i + CHUNKS_AHEAD)
                gelu(0, i)
            for t in range(KT):
                high_fT(1, t)
            with act.Fori(1, BATCH - 1) as b:
                for i in range(CHUNKS):
                    gelu(b, i)
                for t in range(KT):
                    high_fT(b + 1, t)
            for i in range(CHUNKS):
                gelu(BATCH - 1, i)

        @block.tensor
        def _(pe):
            def product(dst, wH, wL, mH, mL, first, last):
                nc.tensor.matmul(dst, wH, mH, start=first, stop=False)
                nc.tensor.matmul(dst, wH, mL, start=False, stop=False)
                return nc.tensor.matmul(dst, wL, mH, start=False, stop=last)

            def take_bank(n):
                if not (isinstance(n[0], int) and use(*n) < 2):
                    pe.wait_ge(g_done, use(*n) - 1)

            def transpose_x(b, t):
                n = use_xT(b, t)
                take_bank(n)
                pe.wait_ge(xn_done, b * KT + (t + 1))
                for k in range(KT):
                    mm = nc.tensor.transpose(G(n)[:, k * P:(k + 1) * P], xn[:, t % 2, k * P:(k + 1) * P], ident[:, :])
                mm.then_inc(g_full, 1)

            def project_QK(b, g, is_k, layer, pieces=range(KT)):
                n = (use_K if is_k else use_Q)(b, g)
                small = layer == CROSS and is_k
                m = WQ2 if layer == CROSS else WK if is_k else WQ
                cols = slice(g * P, (g + 1) * P)
                for k in pieces:
                    if k == 0:
                        take_bank(n)
                        if g == 0:
                            pe.wait_ge(g_done, use(*use_xT(b, KT - 1)) + 1)
                        if g == 0 and small:
                            pe.wait_ge(raw_split, FIRST_CTX if isinstance(b, int) and b == BATCH else b + CTX_OFFSET)
                    if small:
                        mm = product(G(n), WH[:, WKV2, 0, cols], WL[:, WKV2, 0, cols],
                                     WH[:, 0, CTX_SLICE, :], WL[:, 0, CTX_SLICE, :], True, True)
                    else:
                        mm = product(G(n), WH[:, m, k, cols], WL[:, m, k, cols], xTH[:, k, :], xTL[:, k, :],
                                     k == 0, k == KT - 1)
                    if small or k == KT - 1:
                        mm.then_inc(g_full, 1)

            def project_V(b, t, layer, pieces=range(KT)):
                n = use_V(b, t)
                rows = slice(t * P, (t + 1) * P)
                for k in pieces:
                    if k == 0:
                        take_bank(n)
                    if layer == SELF:
                        mm = product(G(n), xTH[:, k, rows], xTL[:, k, rows], WH[:, WV, k, :], WL[:, WV, k, :],
                                     k == 0, k == KT - 1)
                    else:
                        mm = product(G(n), WH[:, 0, CTX_SLICE, rows], WL[:, 0, CTX_SLICE, rows],
                                     WH[:, WKV2, 1, :], WL[:, WKV2, 1, :], True, True)
                    if layer == CROSS or k == KT - 1:
                        mm.then_inc(g_full, 1)

            def project_out(b, t, layer, pieces=range(GROUPS)):
                n = use_Wo(b, t)
                rows = slice(t * P, (t + 1) * P)
                m = WO if layer == SELF else WO2
                for g in pieces:
                    if g == 0:
                        take_bank(n)
                        if t == 0:
                            pe.wait_ge(oL_done, units(b, GROUPS))
                    mm = product(G(n), oTH[:, g, rows], oTL[:, g, rows], WH[:, m, g, :], WL[:, m, g, :],
                                 g == 0, g == GROUPS - 1)
                    if g == GROUPS - 1:
                        mm.then_inc(g_full, 1)

            def scores_for_max(b, g, h, q, layer):
                par = g % 2
                if h == 0 and q == 0:
                    pe.wait_ge(stack_in[par], b * (2 * STACKED) + STACKED * (g // 2 + 1))
                if not (isinstance(b, int) and b == 0 and g == 0 and h == 0 and q < 2):
                    pe.wait_ge(s_done, b * 64 + (16 * g + 4 * h + q - 1))
                n = keys(layer, q)
                dst = PS[:, S_BANK + q % 2, :]
                mm = nc.tensor.matmul(dst[:, 0:n], stackQ[0:STACK, par, h, q * P:(q + 1) * P],
                                      stackK[0:STACK, par, h, 0:n], start=True, stop=layer == SELF)
                if layer == CROSS:
                    mm = nc.tensor.matmul(dst[:, n - P:n], identb[:, :], mask_qk[:, :], start=False, stop=True)
                mm.then_inc(s_full, 1)

            def scores(b, g, k, h, layer):
                par = g % 2
                if k == 0 and h == 0:
                    pe.wait_ge(m_in[par], b * (2 * MAXED) + MAXED * (g // 2 + 1))
                if not (isinstance(b, int) and b == 0 and g == 0 and k == 0 and h < 2):
                    pe.wait_ge(p_ready, b * 64 + (16 * g + 4 * k + h - 1))
                q0 = queries(layer, k)
                dst = PS[:, T_BANK + h % 2, :]
                mm = nc.tensor.matmul(dst[:, q0:SEQ], stackK[0:STACK + 2, par, h, k * P:(k + 1) * P],
                                      stackQ[0:STACK + 2, par, h, q0:SEQ], start=True, stop=layer == SELF)
                if layer == CROSS:
                    mm = nc.tensor.matmul(dst[:, q0:q0 + P], identb[:, :], mask_kq[:, :], start=False, stop=True)
                mm.then_inc(t_full, 1)

            def transpose_max(b, g):
                n = use_m(b, g)
                take_bank(n)
                pe.wait_ge(s_done, b * 64 + 16 * (g + 1))
                nc.tensor.transpose(G(n)[0:HPG * KT, 0:P], m_cols[:, :], ident[:, :]).then_inc(g_full, 1)

            def four_heads(dst, q0, lhs, rhs, first, last):
                for h in range(HPG):
                    mm = nc.tensor.matmul(PS[h * HEAD:(h + 1) * HEAD, dst, q0:SEQ], lhs(h), rhs(h),
                                          start=first, stop=last)
                return mm

            def weigh_values(b, g, k, layer):
                if g == 0:
                    pe.wait_ge(g_done, use(*use_V(b, k)) + 1)
                if k == 0 and not (isinstance(b, int) and b == 0 and g == 0):
                    pe.wait_ge(o_done, units(b, g))
                pe.wait_ge(p_ready, b * 64 + (16 * g + 4 * k + 4))
                q0 = queries(layer, k)
                mm = four_heads(O_BANK, q0, lambda h: V[:, k, (g * HPG + h) * HEAD:(g * HPG + h + 1) * HEAD],
                                lambda h: PT[:, (4 * k + h) % 8, q0:SEQ], k == 0, k == KT - 1)
                if k < KT - 1:
                    mm.then_inc(p_used, 1)

            def sum_rows(b, g, k, layer):
                if k < KT - 1:
                    pe.wait_ge(p_added, b * (GROUPS * ADDS) + ADDS * (g + 1))
                    four_heads(R_BANK, 0, lambda h: ones[:, :], lambda h: P_sum[:, h, :], True, False)
                else:
                    q0 = queries(layer, k)
                    four_heads(R_BANK, q0, lambda h: ones[:, :], lambda h: PT[:, (4 * k + h) % 8, q0:SEQ],
                               False, True).then_inc(p_used, 1)

            pe.wait_ge(consts, 12)
            for t in range(KT):
                transpose_x(0, t)
            pe.wait_ge(w_ready, KT)
            project_QK(0, 0, False, SELF)
            pe.wait_ge(w_ready, 2 * KT)
            project_QK(0, 0, True, SELF)
            pe.wait_ge(w_ready, 3 * KT)
            project_V(0, 0, SELF)
            project_V(0, 1, SELF)
            project_QK(0, 1, False, SELF)
            for h in range(HPG):
                for q in range(KT):
                    scores_for_max(0, 0, h, q, SELF)
                project_QK(0, 1, True, SELF, (h,))
            transpose_max(0, 0)
            project_QK(0, 2, False, SELF)

            def slot(b, g, layer, after):
                layer1, layer2, layer3 = layers_ahead(g, layer, after)
                if isinstance(b, int) and b == 0 and g == 1:
                    pe.wait_ge(w_ready, 4 * KT)
                for _, kind, i, j in pe_order(b, g, layer, after):
                    if kind == "scores":
                        scores(b, g, i, j, layer)
                    elif kind == "values":
                        weigh_values(b, g, i, layer)
                    elif kind == "sums":
                        sum_rows(b, g, i, layer)
                    elif kind == "max":
                        scores_for_max(*following(b, g, 1), i, j, layer1)
                    elif kind == "turn_max":
                        transpose_max(*following(b, g, 1))
                    elif kind == "K":
                        project_QK(*following(b, g, 2), True, layer2, (j,))
                    elif kind == "Q":
                        if j == 0 and layer3 != layer and g == 1:
                            pe.wait_ge(raw_split, KT)
                        project_QK(*following(b, g, 3), False, layer3, (j,))
                    elif kind == "V":
                        project_V(b, i, layer, (j,))
                    elif kind == "V'":
                        project_V(b + 1, i, after, (j,))
                    elif kind == "out":
                        project_out(b - 1, i, SELF if isinstance(b, int) and b == BATCH else layer, (j,))
                    elif kind == "norm":
                        transpose_x(b + 1, i)
                    elif kind == "up":
                        up(0, i, (j,))

            def transpose_f(b, t):
                if isinstance(b, int) and b == 1 and t < 2:
                    pe.wait_ge(g_done, use(*use_Wo(LAST, KT - 1)) + 1)
                else:
                    pe.wait_ge(f_done, b * KT + (t - 1 - KT))
                pe.wait_ge(xn_done, b * KT + (2 * BATCH * KT + t + 1))
                for k in range(KT):
                    mm = nc.tensor.transpose(F(t)[:, k * P:(k + 1) * P], xn[:, t % 2, k * P:(k + 1) * P], ident[:, :])
                mm.then_inc(f_full, 1)

            def up(b, i, pieces=range(KT)):
                j = CHUNK_ORDER[i]
                first = isinstance(b, int) and b == 0
                for k in pieces:
                    if k == 0:
                        if first and i < EARLY:
                            pe.wait_ge(raw_split, RAW_TOTAL - EARLY + i + 1)
                        elif first:
                            pe.wait_ge(fw_ready, i + 1 - EARLY)
                        if first and i == 0:
                            pe.wait_ge(g_done, use(*use_xT(2 * BATCH, KT - 1)) + 1)
                        elif i == 0:
                            pe.wait_ge(f_done, b * KT)
                        if first and i == 2:
                            pe.wait_ge(p_ready, 2 * BATCH * 64)
                        elif not (first and i < FIRST_UPS):
                            pe.wait_ge(h_gelu, b * CHUNKS + (i - 1))
                    cols = slice(k * P, (k + 1) * P)
                    mm = product(H(b, i), FH[:, j, cols], FL[:, j, cols], xTH[:, k, :], xTL[:, k, :],
                                 k == 0, k == KT - 1)
                    if k == KT - 1:
                        mm.then_inc(h_full, 1)

            def down(b, i):
                j = CHUNK_ORDER[i]
                pe.wait_ge(h_ready, b * CHUNKS + (i + 1))
                if i == 0 and isinstance(b, int) and b == 0:
                    pe.wait_ge(h_gelu, FIRST_UPS)
                elif i == 0:
                    pe.wait_ge(y_done, b * KT)
                for t in range(KT):
                    rows = slice(t * P, (t + 1) * P)
                    mm = product(PS[:, ACC_BANK + t, :], hidH[:, i % 2, rows], hidL[:, i % 2, rows],
                                 FH[:, j, DIM:CHUNK], FL[:, j, DIM:CHUNK], i == 0, i == CHUNKS - 1)
                mm.then_inc(h_used, 1)

            batches(pe, slot)

            def ffn_batch(b, first, last):
                for i in range(FIRST_UPS if first else 0, CHUNKS):
                    up(b, i)
                    if i == CHUNKS - 1 and not last:
                        transpose_f(b + 1, 0)
                        transpose_f(b + 1, 1)
                    if i:
                        down(b, i - 1)
                if not last:
                    transpose_f(b + 1, 2)
                    transpose_f(b + 1, 3)
                down(b, CHUNKS - 1)

            for i in range(2, FIRST_UPS):
                up(0, i)
            for t in range(KT):
                project_out(LAST, t, CROSS)
            for i in range(FIRST_UPS - 1):
                down(0, i)
            ffn_batch(0, True, False)
            with pe.Fori(1, BATCH - 1) as b:
                ffn_batch(b, False, False)
            ffn_batch(BATCH - 1, False, True)

        @block.vector
        def _(dve):
            def low_weight(m, buf, k):
                dve.wait_ge(wH_ready, m * KT + k + 1)
                nc.vector.tensor_tensor(WL[:, m, k, :], buf[:, k, :], WH[:, m, k, :].bitcast(F32),
                                        ALU.subtract).then_inc(w_ready, 1)

            def row_of(b, layer):
                return b * KT - layer * BATCH * KT

            def norm_stats(t, first_row):
                nc.vector.bn_stats(stats[:, t, :], residual(first_row + t)).then_inc(stats_done, 1)

            def norm_aggregate(b):
                dve.wait_ge(stats_done, b * KT + KT)
                nc.vector.memset(spare[:, :], 0.0).then_inc(spare_done, 1)
                for t in range(KT):
                    nc.vector.bn_aggr(mv[:, t, :], stats[:, t, :]).then_inc(mv_done, 1)

            def norm_moments(b, first_row):
                for t in range(KT):
                    norm_stats(t, first_row)
                norm_aggregate(b)

            def normed(b, t, first_row):
                if t == 0:
                    dve.wait_ge(rstd_done, b + 1)
                nc.vector.tensor_scalar(xn[:, t % 2, :], residual(first_row + t), mv[:, t, 0:1], rstd[:, t:t + 1],
                                        ALU.subtract, ALU.mult).then_inc(xn_done, 1)

            def low_xT(b, t):
                n = use_xT(b, t)
                dve.wait_ge(g_high, high_count(*n))
                nc.vector.tensor_tensor(xTL[:, :, t * P:(t + 1) * P], G(n).rearrange("p (k n) -> p k n", k=KT),
                                        xTH[:, :, t * P:(t + 1) * P].bitcast(F32), ALU.subtract).then_inc(g_done, 1)

            def low_QK(b, g, is_k, layer):
                n = (use_K if is_k else use_Q)(b, g)
                dve.wait_ge(g_high, high_count(*n))
                if layer == SELF:
                    nc.vector.scalar_tensor_tensor(out=stL, in0=G(n), scalar=(bkc if is_k else bqc)[:, g:g + 1],
                                                   in1=stH.bitcast(F32), op0=ALU.add,
                                                   op1=ALU.subtract).then_inc(g_done, 1)
                else:
                    nc.vector.tensor_tensor(stL, G(n), stH.bitcast(F32), ALU.subtract).then_inc(g_done, 1)

            def take_V(b, t, layer):
                n = use_V(b, t)
                dve.wait_ge(g_full, use(*n) + 1)
                if layer == SELF:
                    nc.vector.tensor_tensor(V[:, t, :], G(n), bv_b, ALU.add).then_inc(g_done, 1)
                else:
                    nc.vector.tensor_copy(V[:, t, :], G(n)).then_inc(g_done, 1)

            def add_residual(b, t, layer):
                n = use_Wo(b, t)
                dve.wait_ge(g_full, use(*n) + 1)
                if layer == SELF:
                    dve.wait_ge(bo_added, b * KT + (t + 1))
                tile = residual(row_of(b, layer) + t)
                nc.vector.tensor_tensor(tile, tile, G(n), ALU.add).then_inc(g_done, 1)

            def maximum(b, g, h, q, layer):
                dve.wait_ge(s_full, b * 64 + (16 * g + 4 * h + q + 1))
                nc.vector.tensor_reduce(m_cols[:, h * KT + q:h * KT + q + 1],
                                        PS[:, S_BANK + q % 2, 0:keys(layer, q)], AX.X, ALU.max).then_inc(s_done, 1)

            def take_max(b, g):
                n = use_m(b, g)
                dve.wait_ge(g_full, use(*n) + 1)
                if not (isinstance(b, int) and b == 0 and g == 0):
                    pb, pg = preceding(b, g)
                    dve.wait_ge(m_in[pg % 2], pb * (2 * MAXED) + MAXED * (pg // 2 + 1))
                rows = G(n)[0:HPG * KT, 0:P]
                nc.vector.tensor_scalar(m_row[:, 0, :], rows, -1.0, None, ALU.mult).then_inc(m_high, 1)
                dve.wait_ge(m_high, units(b, g) + 1)
                nc.vector.scalar_tensor_tensor(out=m_row[:, 1, :], in0=rows, scalar=-1.0,
                                               in1=m_row[:, 0, :].bitcast(F32), op0=ALU.mult,
                                               op1=ALU.subtract).then_inc(g_done, 1)

            def divide(b, g):
                dve.wait_ge(p_used, b * 16 + (4 * g + 4))
                if not (isinstance(b, int) and b == 0 and g == 0):
                    dve.wait_ge(oL_done, units(b, g))
                nc.vector.reciprocal(oT[:, :], PS[:, R_BANK, :]).then_inc(r_done, 1)
                dve.wait_ge(r_done, units(b, g) + 1)
                nc.vector.tensor_tensor(oT[:, :], PS[:, O_BANK, :], oT[:, :], ALU.mult).then_inc(o_done, 1)

            dve.wait_ge(x_loaded, DMA)
            norm_moments(0, 0)
            normed(0, 0, 0)
            normed(0, 1, 0)
            for k in range(KT):
                low_weight(WQ, PT[:, 0:4, :], k)
            low_xT(0, 0)
            normed(0, 2, 0)
            low_xT(0, 1)
            normed(0, 3, 0)
            low_xT(0, 2)
            low_xT(0, 3)
            for k in range(KT):
                low_weight(WK, PT[:, 4:8, :], k)
            dve.wait_ge(small_loaded, DMA * SMALL)
            low_QK(0, 0, False, SELF)
            for k in range(KT):
                low_weight(WV, V, k)
            low_QK(0, 0, True, SELF)
            take_V(0, 0, SELF)
            take_V(0, 1, SELF)
            for k in range(KT):
                low_weight(WO, PT[:, 0:4, :], k)
            low_QK(0, 1, False, SELF)
            for h in range(HPG):
                for q in range(KT):
                    maximum(0, 0, h, q, SELF)
            low_QK(0, 1, True, SELF)
            take_max(0, 0)
            low_QK(0, 2, False, SELF)

            def slot(b, g, layer, after):
                layer1, layer2, layer3 = layers_ahead(g, layer, after)
                places = PLACES[layer]
                lag = places["lag"]
                work = [piece for piece in pe_order(b, g, layer, after) if piece[1] in ("max", "turn_max")]
                work.append((places["divide"], "divide", 0, 0))
                if layer2 is not None:
                    work.append((places["K"][g][1] + lag, "K", 0, 0))
                if layer3 is not None:
                    work.append((places["Q"][g][1] + lag, "Q", 0, 0))
                if g == 0:
                    work += [(places["V_here"][t][1] + lag, "V", 2 + t, 0) for t in range(2)]
                    if has_before(b):
                        work += [(out_place(places, t + 1), "out", t, 0) for t in range(KT)]
                    work += [(places["stats"][t], "stats", t, 0) for t in range(KT)]
                    work.append((places["aggregate"], "aggregate", 0, 0))
                    work += [(places["normed"][t], "normed", t, 0) for t in range(2)]
                if g == 1:
                    work += [(places["norm"][t] + lag, "norm", t, 0) for t in range(KT)]
                    work += [(places["norm"][t] + lag, "normed", t + 2, 0) for t in range(2)]
                if g == GROUPS - 1 and after != FFN:
                    work += [(places["V_next"][t][1] + lag, "V'", t, 0) for t in range(2)]
                for _, kind, i, j in sorted(work, key=lambda piece: piece[0]):
                    if kind == "max":
                        maximum(*following(b, g, 1), i, j, layer1)
                    elif kind == "turn_max":
                        take_max(*following(b, g, 1))
                    elif kind == "divide":
                        divide(b, g)
                    elif kind == "K":
                        low_QK(*following(b, g, 2), True, layer2)
                    elif kind == "Q":
                        low_QK(*following(b, g, 3), False, layer3)
                    elif kind == "V":
                        take_V(b, i, layer)
                    elif kind == "V'":
                        take_V(b + 1, i, after)
                    elif kind == "out":
                        add_residual(b - 1, i, SELF if isinstance(b, int) and b == BATCH else layer)
                    elif kind == "stats":
                        if i == 0 and isinstance(b, int) and b == 0:
                            dve.wait_ge(x_rest_loaded, DMA)
                        if i == 0 and after != SELF:
                            dve.wait_ge(g_done, use(*use_Wo(b - (BATCH - 1), KT - 1)) + 1)
                        norm_stats(i, row_of(b + 1, after))
                    elif kind == "aggregate":
                        norm_aggregate(b + 1)
                    elif kind == "normed":
                        normed(b + 1, i, row_of(b + 1, after))
                    elif kind == "norm":
                        low_xT(b + 1, i)

            batches(dve, slot)

            def low_chunk(i):
                dve.wait_ge(fwH_ready, i + 1 - EARLY)
                j = CHUNK_ORDER[i]
                nc.vector.tensor_tensor(FL[:, j, :], fraw(i), FH[:, j, :].bitcast(F32),
                                        ALU.subtract).then_inc(fw_ready, 1)

            def low_fT(b, t):
                dve.wait_ge(f_high, b * KT + (t + 1 - KT))
                nc.vector.tensor_tensor(xTL[:, :, t * P:(t + 1) * P], F(t).rearrange("p (k n) -> p k n", k=KT),
                                        xTH[:, :, t * P:(t + 1) * P].bitcast(F32), ALU.subtract).then_inc(f_done, 1)

            def split_hidden(b, i):
                dve.wait_ge(h_gelu, b * CHUNKS + (i + 1))
                if not (isinstance(b, int) and b == 0 and i < 2):
                    dve.wait_ge(h_used, b * CHUNKS + (i - 1))
                nc.vector.tensor_copy(hidH[:, i % 2, :], hid[:, i % 2, :]).then_inc(h_high, 1)
                dve.wait_ge(h_high, b * CHUNKS + (i + 1))
                nc.vector.tensor_tensor(hidL[:, i % 2, :], hid[:, i % 2, :], hidH[:, i % 2, :].bitcast(F32),
                                        ALU.subtract).then_inc(h_ready, 1)

            def norm_first(b):
                for t in (0, 1):
                    normed(b + 2 * BATCH, t, b * KT)

            def norm_transposed(b):
                for t in range(KT):
                    low_fT(b, t)
                    if t < 2:
                        normed(b + 2 * BATCH, t + 2, b * KT)

            def take_out(b):
                dve.wait_ge(h_used, b * CHUNKS + CHUNKS)
                for t in range(KT):
                    dve.wait_ge(b2_added, b * KT + (t + 1))
                    tile = residual(b * KT + t)
                    nc.vector.tensor_tensor(tile, tile, PS[:, ACC_BANK + t, :], ALU.add).then_inc(y_done, 1)

            def ffn_batch(b, first, last):
                for i in range(CHUNKS):
                    if first and i == 2:
                        for t in range(KT):
                            add_residual(LAST, t, CROSS)
                    if first and i >= FIRST_UPS and i + CHUNKS_AHEAD < CHUNKS:
                        low_chunk(i + CHUNKS_AHEAD)
                    if i == 8 and not last:
                        norm_moments(b + (2 * BATCH + 1), b * KT + KT)
                    if i == CHUNKS - 1 and not last:
                        norm_first(b + 1)
                    split_hidden(b, i)
                if not last:
                    norm_transposed(b + 1)
                take_out(b)

            ffn_batch(0, True, False)
            with dve.Fori(1, BATCH - 1) as b:
                ffn_batch(b, False, False)
            ffn_batch(BATCH - 1, False, True)


_WEIGHTS = ("L0_attn_wq", "L0_attn_wk", "L0_attn_wv", "L0_attn_wo")


def kernel(**inputs):
    import numpy as np
    import concourse.bacc as bacc
    from concourse.bass_utils import run_bass_kernel_spmd

    def rows(name):
        return np.ascontiguousarray(np.broadcast_to(np.asarray(inputs[name]), (P, DIM)))

    def columns(name):
        return np.ascontiguousarray(np.asarray(inputs[name]).reshape(-1, P).T)

    def turned(name):
        return np.ascontiguousarray(np.swapaxes(np.asarray(inputs[name]), -1, -2))

    arrays = {
        "x": np.ascontiguousarray(inputs["x"]),
        "ctxT": turned("ctx_512"),
        "wT": np.stack([np.asarray(inputs[n]).T for n in _WEIGHTS]),
        "bq": columns("L0_attn_bq"),
        "bk": columns("L0_attn_bk"),
        "bv": rows("L0_attn_bv"),
        "bo": rows("L0_attn_bo"),
        "wq2T": turned("L0_xattn_Wq"),
        "wkv2T": turned("L0_xattn_Wkv_expand"),
        "wo2T": turned("L0_xattn_Wout"),
        "p1T": turned("L0_ffn_proj1"),
        "b1": columns("L0_ffn_proj1_bias"),
        "p2T": turned("L0_ffn_proj2"),
        "b2": rows("L0_ffn_proj2_bias"),
    }
    nc = bacc.Bacc("TRN2", target_bir_lowering=False, num_devices=1)
    args = [nc.dram_tensor(n, a.shape, mybir.dt.from_np(a.dtype), kind="ExternalInput").ap() for n, a in arrays.items()]
    out = nc.dram_tensor("out", (BATCH, SEQ, DIM), F32, kind="ExternalOutput").ap()
    scratch = nc.dram_tensor("scratch", (2, 2, 2, HEAD, HPG, SEQ), F32, kind="Internal").ap()
    decoder_layer(nc, *args, out, scratch)
    r = run_bass_kernel_spmd(nc, [arrays], core_ids=[0])
    return r.results[0]["out"]
```
